# Optimizing a Trainium2 kernel written in Bass

```python
import numpy as np
import jax
import jax.numpy as jnp

def _softmax(x, axis=-1):
    return jax.nn.softmax(x, axis=axis)

def _gelu(x):
    return jax.nn.gelu(x, approximate=True)

def _silu(x):
    return jax.nn.silu(x)

def _sigmoid(x):
    return jax.nn.sigmoid(x)

def _layernorm(x, axis=-1, eps=1e-05):
    m = jnp.mean(x, axis=axis, keepdims=True)
    v = jnp.var(x, axis=axis, keepdims=True)
    return (x - m) / jnp.sqrt(v + eps)

def _scatter_add(tgt, idx, src, axis=0):
    return tgt.at[idx].add(src)

def _segment_sum(src, seg, n):
    return jax.ops.segment_sum(src, seg, n)
kernel_name = 'mk_sandwich_d1_jaxref_r8_b82401'

def setup_inputs(seed: int=0):
    np.random.seed(seed)
    _w = jnp.asarray

    def _L0_attn_setup():
        import jax, jax.numpy as jnp
        import numpy as np
        BATCH, SEQ, HIDDEN = (2, 512, 512)
        HEADS, HEAD_DIM, BLOCK = (32, 128, 32)
        LAYER_IDX, N_LAYERS = (1, 32)
        EPS = 1e-05

        def _decays():
            base = 1.0 / 2.0 ** (8.0 / HEADS)
            exponent = jnp.arange(HEADS, dtype=jnp.float32) + 1.0
            factor = 1.0 - LAYER_IDX / (N_LAYERS - 1 + 1e-05) + 1e-05
            slope = (base ** exponent * factor)[:, None, None]
            r = jnp.arange(BLOCK, dtype=jnp.float32) + 1.0
            q_decay = jnp.exp(-slope * r[:, None])
            k_decay = jnp.exp(-slope * (BLOCK - r)[:, None])
            diff = r[:, None] - r[None, :]
            diag = slope[None] * diff[None, None]
            diag = jnp.where(diag >= 0, -diag, -jnp.inf)
            diag_decay = jnp.exp(diag)
            block_decay = jnp.exp(-slope * BLOCK)
            return (q_decay, k_decay, diag_decay, block_decay)
        key = jax.random.key(seed)
        ks = jax.random.split(key, 5)
        s = 0.02
        return {'hidden_states': jax.random.normal(ks[0], (BATCH, SEQ, HIDDEN), jnp.float32), 'qkv_w': jax.random.normal(ks[1], (3 * HEADS * HEAD_DIM, HIDDEN), jnp.float32) * s, 'out_w': jax.random.normal(ks[2], (HIDDEN, HEADS * HEAD_DIM), jnp.float32) * s, 'gate_w': jax.random.normal(ks[3], (HEADS * HEAD_DIM, HIDDEN), jnp.float32) * s, 'norm_w': jnp.ones((HEADS * HEAD_DIM,), jnp.float32)}
    _L0_attn_in = _L0_attn_setup()

    def _L0_ffn_setup():
        import jax, jax.numpy as jnp
        import numpy as np
        H, FF = (512, 1792)
        B, S = (4, 256)
        key = jax.random.key(seed)
        ks = jax.random.split(key, 7)
        x = jax.random.normal(ks[0], (B, S, H), dtype=jnp.float32)
        gate_t = jax.random.randint(ks[1], (FF, H), -1, 2, dtype=jnp.int32)
        up_t = jax.random.randint(ks[2], (FF, H), -1, 2, dtype=jnp.int32)
        down_t = jax.random.randint(ks[3], (H, FF), -1, 2, dtype=jnp.int32)
        gate_s = jax.random.uniform(ks[4], (FF,), jnp.float32, 0.01, 0.1)
        up_s = jax.random.uniform(ks[5], (FF,), jnp.float32, 0.01, 0.1)
        down_s = jax.random.uniform(ks[6], (H,), jnp.float32, 0.01, 0.1)
        return {'x': x, 'gate_t': gate_t, 'up_t': up_t, 'down_t': down_t, 'gate_s': gate_s, 'up_s': up_s, 'down_s': down_s}
    _L0_ffn_in = _L0_ffn_setup()
    _d = {'L0_attn_hidden_states': _L0_attn_in['hidden_states'], 'L0_attn_qkv_w': _L0_attn_in['qkv_w'], 'L0_attn_out_w': _L0_attn_in['out_w'], 'L0_attn_gate_w': _L0_attn_in['gate_w'], 'L0_attn_norm_w': _L0_attn_in['norm_w'], 'L0_ffn_gate_t': _L0_ffn_in['gate_t'], 'L0_ffn_up_t': _L0_ffn_in['up_t'], 'L0_ffn_down_t': _L0_ffn_in['down_t'], 'L0_ffn_gate_s': _L0_ffn_in['gate_s'], 'L0_ffn_up_s': _L0_ffn_in['up_s'], 'L0_ffn_down_s': _L0_ffn_in['down_s']}
    _x0 = _d['L0_attn_hidden_states']
    _d['L0_attn_hidden_states'] = jax.random.normal(jax.random.fold_in(jax.random.key(seed), 1), (2, 1024, 512), dtype=_x0.dtype)
    del _x0
    return _d

def reference(L0_attn_hidden_states, L0_attn_qkv_w, L0_attn_out_w, L0_attn_gate_w, L0_attn_norm_w, L0_ffn_gate_t, L0_ffn_up_t, L0_ffn_down_t, L0_ffn_gate_s, L0_ffn_up_s, L0_ffn_down_s):

    def _L0_attn_ref(hidden_states, qkv_w, out_w, gate_w, norm_w):
        import jax, jax.numpy as jnp
        import numpy as np
        BATCH, SEQ, HIDDEN = (2, 512, 512)
        HEADS, HEAD_DIM, BLOCK = (32, 128, 32)
        LAYER_IDX, N_LAYERS = (1, 32)
        EPS = 1e-05

        def _decays():
            base = 1.0 / 2.0 ** (8.0 / HEADS)
            exponent = jnp.arange(HEADS, dtype=jnp.float32) + 1.0
            factor = 1.0 - LAYER_IDX / (N_LAYERS - 1 + 1e-05) + 1e-05
            slope = (base ** exponent * factor)[:, None, None]
            r = jnp.arange(BLOCK, dtype=jnp.float32) + 1.0
            q_decay = jnp.exp(-slope * r[:, None])
            k_decay = jnp.exp(-slope * (BLOCK - r)[:, None])
            diff = r[:, None] - r[None, :]
            diag = slope[None] * diff[None, None]
            diag = jnp.where(diag >= 0, -diag, -jnp.inf)
            diag_decay = jnp.exp(diag)
            block_decay = jnp.exp(-slope * BLOCK)
            return (q_decay, k_decay, diag_decay, block_decay)
        b, s, _ = hidden_states.shape
        h, d, bs = (HEADS, HEAD_DIM, BLOCK)
        nb = s // bs
        q_decay, k_decay, diag_decay, block_decay = _decays()
        qkv = jax.nn.silu(hidden_states @ qkv_w.T)
        qkv = qkv.reshape(b, s, h, 3, d)
        q = jnp.moveaxis(qkv[:, :, :, 0], 2, 1)
        k = jnp.moveaxis(qkv[:, :, :, 1], 2, 1)
        v = jnp.moveaxis(qkv[:, :, :, 2], 2, 1)

        def to_blocks(x):
            return jnp.moveaxis(x.reshape(b, h, nb, bs, d), 2, 0)
        qb, kb, vb = (to_blocks(q), to_blocks(k), to_blocks(v))

        def step(kv, blk):
            cq, ck, cv = blk
            scores = jnp.einsum('bhnd,bhmd->bhnm', cq, ck) * diag_decay
            intra = jnp.einsum('bhnm,bhmd->bhnd', scores, cv)
            inter = jnp.einsum('bhnd,bhde->bhne', cq * q_decay, kv)
            kv_next = kv * block_decay + jnp.einsum('bhnd,bhne->bhde', ck * k_decay, cv)
            return (kv_next, intra + inter)
        kv0 = jnp.zeros((b, h, d, d), hidden_states.dtype)
        _, out_blocks = jax.lax.scan(step, kv0, (qb, kb, vb))
        attn = jnp.moveaxis(out_blocks, 0, 2)
        attn = attn.reshape(b, h, s, d).transpose(0, 2, 1, 3).reshape(b, s, h * d)
        xf = attn.astype(jnp.float32)
        xf = xf * jax.lax.rsqrt(jnp.mean(xf * xf, axis=-1, keepdims=True) + EPS)
        normed = norm_w * xf.astype(attn.dtype)
        gate = jax.nn.sigmoid(hidden_states @ gate_w.T)
        return gate * normed @ out_w.T

    def _L0_ffn_ref(x, gate_t, up_t, down_t, gate_s, up_s, down_s):
        import jax, jax.numpy as jnp
        import numpy as np
        H, FF = (512, 1792)
        B, S = (4, 256)
        Bb, Ss, Hh = x.shape
        x_flat = x.reshape(Bb * Ss, Hh)
        gate_w = gate_t.astype(jnp.float32) * gate_s[:, None]
        up_w = up_t.astype(jnp.float32) * up_s[:, None]
        down_w = down_t.astype(jnp.float32) * down_s[:, None]
        gate_out = x_flat @ gate_w.T
        up_out = x_flat @ up_w.T
        hidden = jax.nn.silu(gate_out) * up_out
        out_flat = hidden @ down_w.T
        return out_flat.reshape(Bb, Ss, -1)
    x = L0_attn_hidden_states
    x = x + _layernorm(_L0_attn_ref(_layernorm(x, axis=-1), L0_attn_qkv_w, L0_attn_out_w, L0_attn_gate_w, L0_attn_norm_w), axis=-1)
    x = x + _layernorm(_L0_ffn_ref(_layernorm(x, axis=-1), L0_ffn_gate_t, L0_ffn_up_t, L0_ffn_down_t, L0_ffn_gate_s, L0_ffn_up_s, L0_ffn_down_s), axis=-1)
    return x

_drawn_inputs = setup_inputs


def setup_inputs(seed=0):
    import zlib

    import numpy as np

    out = dict(_drawn_inputs(seed))
    spreads = {'L0_attn_norm_w': (1.0, 0.2)}
    factors = {}
    for name, (base, spread) in spreads.items():
        noise = np.random.default_rng([zlib.crc32(name.encode()), seed]).standard_normal(out[name].shape)
        drawn = base * np.exp(spread * noise) if base else spread * noise
        out[name] = jnp.asarray(drawn.astype(out[name].dtype))
    for name, factor in factors.items():
        out[name] = (out[name] * factor).astype(out[name].dtype)
    return out
```

```python
from contextlib import ExitStack

import concourse.bass as bass
from concourse import mybir
from concourse.alu_op_type import AluOpType as ALU

P = 128
BATCH, SEQ, HID = 2, 1024, 512
TOK = BATCH * SEQ
HEADS, HD = 32, 128
FF = 1792
LN_EPS = 1e-5
RMS_EPS = 1e-5

SEG = 512
NSEG = TOK // SEG
SEGS_PER_BATCH = SEQ // SEG
CH = SEG // P
TILES = TOK // P
HT = HID // P
PAIRS = HEADS // 2
STEPS = PAIRS * NSEG
KK, QQ, VV, GG = range(4)
TAB_D, TAB_Q, TAB_K, TAB_B = 0, 2 * P, 4 * P, 4 * P + 2
TAB = 4 * P + 4

FG = FF // (2 * P)
FSTEPS = FG * NSEG
GU_INTS = 2 * FF * HID
WIDTH_CHECKS = 3 * FF * HID // (P * HID)
CHECKS_PER_PAIR = 3
CHECK_PAIRS = WIDTH_CHECKS // CHECKS_PER_PAIR
F32R_EXACT = 2.0 ** 12

ACT = mybir.ActivationFunctionType
AX = mybir.AxisListType
F32 = mybir.dt.float32
F32R = mybir.dt.float32r
I32 = mybir.dt.int32


def wait(eng, sem, value):
    if isinstance(value, int) and value <= 0:
        return
    eng.wait_ge(sem, value)


def states_before(a, odd):
    return 7 * a + (1 if odd else 0)


def sandwich_kernel(nc, x, w_attn, w_out, norm_w, tables, w_ints, ffn_scales, down_s, out):
    ctx = ExitStack()
    with ctx:
        def sem(name):
            return ctx.enter_context(nc.semaphore(name))

        def sb(name, shape, dt=F32, scope=ctx):
            return scope.enter_context(nc.sbuf_tensor(name, shape, dt))

        x_hi = sb("x_hi", [P, HT, TOK], F32R)
        x_lo = sb("x_lo", [P, HT, TOK], F32R)
        y = sb("y", [P, TILES, HID])
        sumsq = sb("sumsq", [P, TOK])
        sq = sb("sq", [P, 2, SEG])
        ident = sb("ident", [P, P])
        ones = sb("ones", [P, 1])
        stats = sb("stats", [P, CH, 6])
        meanvar = sb("meanvar", [P, CH, 2])
        var_eps = sb("var_eps", [P, CH])
        stdev = sb("stdev", [P, CH])
        rstd = sb("rstd", [P, CH])
        rms_term = sb("rms_term", [P, TILES])
        block_max = sb("block_max", [P, CHECKS_PER_PAIR])
        ints_max = sb("ints_max", [P, CHECKS_PER_PAIR])
        part_max = sb("part_max", [P, 1])
        all_max = sb("all_max", [P, 1])
        wide = sb("wide", [P, 1], I32)

        def bank(name):
            return ctx.enter_context(nc.psum_tensor(name, [P, SEG], F32))

        proj_ps = [bank("proj_ps0"), bank("proj_ps1")]
        kt_at = [bank("kt_at0"), bank("kt_at1")]
        sc_st = [bank("sc_st0"), bank("sc_st1")]
        yp = [bank("yp0"), bank("yp1")]
        ln1_ring = kt_at + sc_st + yp

        x_in = [sem(f"x_in{s}") for s in range(NSEG)]
        raw_in = [sem("raw_in0"), sem("raw_in1")]
        table_in, ow_in, norm_in = sem("table_in"), sem("ow_in"), sem("norm_in")
        const_done = sem("const_done")
        ln_own = sem("ln_own")
        var_ready = sem("var_ready")
        sd_ready = sem("sd_ready")
        normed = sem("normed")
        xt_done = sem("xt_done")
        xhi_done = sem("xhi_done")
        xlo_done = sem("xlo_done")
        y_cleared = sem("y_cleared")
        ss_cleared = sem("ss_cleared")
        whi_done, wlo_done = sem("whi_done"), sem("wlo_done")
        ow_scaled, owhi_done, owlo_done = sem("ow_scaled"), sem("owhi_done"), sem("owlo_done")
        table_ready = sem("table_ready")
        proj_done = sem("proj_done")
        kt_done = sem("kt_done")
        score_done = sem("score_done")
        contrib_done = sem("contrib_done")
        attn_done = sem("attn_done")
        yproj_done = sem("yproj_done")
        sig_done = sem("sig_done")
        kd_done = sem("kd_done")
        sq_done = sem("sq_done")
        ghi_done = sem("ghi_done")
        silu_done = sem("silu_done")
        pdec_done = sem("pdec_done")
        state_done = sem("state_done")
        gated_done = sem("gated_done")
        yacc_done = sem("yacc_done")
        qd_done = sem("qd_done")
        ss_done = sem("ss_done")
        glo_done = sem("glo_done")
        check_in = sem("check_in")
        max_cleared = sem("max_cleared")
        block_done = sem("block_done")
        max_done = sem("max_done")
        part_done = sem("part_done")
        all_max_done = sem("all_max_done")
        wide_ready = sem("wide_ready")
        ssum_done = sem("ssum_done")
        xres_in = sem("xres_in")
        ds_in = sem("ds_in")
        fraw_in, draw_in, fs_in = sem("fraw_in"), sem("draw_in"), sem("fs_in")
        fs_ready = sem("fs_ready")
        fhi_done, flo_done = sem("fhi_done"), sem("flo_done")
        dhi_done, dlo_done = sem("dhi_done"), sem("dlo_done")
        fproj_done = sem("fproj_done")
        fsig_done = sem("fsig_done")
        fgate_done = sem("fgate_done")
        hid_done = sem("hid_done")
        hhi_done, hlo_done = sem("hhi_done"), sem("hlo_done")
        down_done = sem("down_done")
        y2_cleared = sem("y2_cleared")
        y2acc_done = sem("y2acc_done")
        final_done = sem("final_done")
        out_sent = sem("out_sent")

        two = ExitStack()
        raw = sb("raw", [P, 2, HT, 2, P], scope=two)
        w_hi = sb("w_hi", [P, 4, HT, 2, P], F32R, two)
        w_lo = sb("w_lo", [P, 4, HT, 2, P], F32R, two)
        ow = sb("ow", [P, 2, HID], scope=two)
        ow_hi = sb("ow_hi", [P, 2, HID], F32R, two)
        ow_lo = sb("ow_lo", [P, 2, HID], F32R, two)
        nw = sb("nw", [P, 2], scope=two)
        table_stage = sb("table_stage", [P, TAB], scope=two)
        table = sb("table", [P, TAB], scope=two)
        k = sb("k", [P, 2, SEG], scope=two)
        q = sb("q", [P, 2, SEG], scope=two)
        qd = sb("qd", [P, 2, SEG], scope=two)
        g = sb("g", [P, 2, SEG], scope=two)
        v = sb("v", [P, CH, 2, HD], scope=two)
        kd = sb("kd", [P, 2, CH, HD], scope=two)
        pd = sb("pd", [P, 2, CH, P], scope=two)
        state = sb("state", [P, 2, CH, HD], scope=two)
        g_hi = sb("g_hi", [P, 2, SEG], F32R, two)
        g_lo = sb("g_lo", [P, 2, SEG], F32R, two)
        check = sb("check", [P, HID], I32, two)
        two.close()

        three = ExitStack()
        xres = sb("xres", [P, CH, HID], scope=three)
        f_hi = sb("f_hi", [P, 2, 2, HT, P], F32R, three)
        f_lo = sb("f_lo", [P, 2, 2, HT, P], F32R, three)
        fraw = sb("fraw", [P, 2, 2, HT, P], I32, three)
        d_hi = sb("d_hi", [P, 2, HID], F32R, three)
        d_lo = sb("d_lo", [P, 2, HID], F32R, three)
        draw = sb("draw", [P, 2, HID], I32, three)
        fs_stage = sb("fs_stage", [P, 4], scope=three)
        fs = sb("fs", [P, 4], scope=three)
        ds = sb("ds", [P, HID], scope=three)
        y2 = sb("y2", [P, TILES, HID], scope=three)
        xn = y2[:, TILES - CH:TILES]
        hid = sb("hid", [P, 2, SEG], scope=three)
        h_hi = sb("h_hi", [P, 2, 2, SEG], F32R, three)
        h_lo = sb("h_lo", [P, 2, 2, SEG], F32R, three)
        three.close()

        ffn_ps = [proj_ps[0], proj_ps[1], kt_at[0], kt_at[1]]
        w_ffn = w_ints[0:GU_INTS].rearrange("(g p t u r f) -> g p t u r f", p=P, t=2, u=2, r=HT, f=P)
        w_down = w_ints[GU_INTS:].rearrange("(g p f n) -> g p f n", p=P, f=2, n=HID)
        w_blocks = w_ints.rearrange("(c p n) -> c p n", p=P, n=HID)
        x_tiles = x.rearrange("(s t p) h -> s p t h", t=CH, p=P)
        out_tiles = out.rearrange("(s t p) h -> s p t h", t=CH, p=P)
        block = ctx.enter_context(nc.Block())

        def tokens(seg):
            return slice(seg * SEG, (seg + 1) * SEG)

        def chunk(c):
            return slice(c * P, (c + 1) * P)

        @block.sync
        def _(sp):
            def attn_weights(p, kind):
                wait(sp, wlo_done, 4 * p + kind - 1)
                sp.dma_start(raw[:, kind % 2], w_attn[p, kind]).then_inc(raw_in[kind % 2], 16)

            def pair_tables(p):
                wait(sp, table_ready, p)
                sp.dma_start(table_stage[:, :], tables[p]).then_inc(table_in, 16)

            def pair_out_weights(p):
                wait(sp, owlo_done, p)
                sp.dma_start(ow[:, :, :], w_out[p]).then_inc(ow_in, 16)
                sp.dma_start(nw[:, :], norm_w[p]).then_inc(norm_in, 16)

            sp.dma_start(y[:, 0:CH], x_tiles[0]).then_inc(x_in[0], 16)
            attn_weights(0, KK)
            attn_weights(0, QQ)
            sp.dma_start(y[:, CH:2 * CH], x_tiles[1]).then_inc(x_in[1], 16)
            attn_weights(0, VV)
            attn_weights(0, GG)
            sp.dma_start(y[:, 2 * CH:3 * CH], x_tiles[2]).then_inc(x_in[2], 16)
            sp.dma_start(y[:, 3 * CH:4 * CH], x_tiles[3]).then_inc(x_in[3], 16)
            pair_tables(0)
            pair_out_weights(0)
            with sp.Fori(1, PAIRS) as p:
                attn_weights(p, KK)
                attn_weights(p, QQ)
                pair_tables(p)
                pair_out_weights(p)
                attn_weights(p, VV)
                attn_weights(p, GG)

            sp.wait_ge(wlo_done, 4 * PAIRS)
            sp.dma_start(xres[:, :, :], x_tiles[0]).then_inc(xres_in, 16)

            def ffn_weights(n):
                wait(sp, flo_done, 2 * n)
                sp.dma_start(fraw[:, :, :, :, :], w_ffn[n]).then_inc(fraw_in, 16)
                wait(sp, dlo_done, n)
                sp.dma_start(draw[:, :, :], w_down[n]).then_inc(draw_in, 16)
                wait(sp, fs_ready, n)
                sp.dma_start(fs_stage[:, :], ffn_scales[n]).then_inc(fs_in, 16)

            sp.wait_ge(yacc_done, 4 * STEPS)
            sp.wait_ge(ss_done, 2 * STEPS)
            ffn_weights(0)
            sp.dma_start(ds[:, :], down_s.partition_broadcast(P)).then_inc(ds_in, 16)
            for s in range(1, NSEG):
                sp.wait_ge(normed, TILES + 2 * CH * s - CH + 1)
                sp.dma_start(xres[:, :, :], x_tiles[s]).then_inc(xres_in, 16)
            with sp.Fori(1, FG) as n:
                ffn_weights(n)
            for s in range(NSEG):
                sp.wait_ge(final_done, CH * (s + 1))
                sp.dma_start(out_tiles[s], y[:, s * CH:(s + 1) * CH]).then_inc(out_sent, 16)
            sp.wait_ge(out_sent, 16 * NSEG)

        @block.gpsimd
        def _(pool):
            def split_lo(p, kind):
                pool.wait_ge(whi_done, 4 * p + kind + 1)
                pool.tensor_tensor(w_lo[:, kind], raw[:, kind % 2], w_hi[:, kind].bitcast(F32),
                                   ALU.subtract).then_inc(wlo_done, 1)

            def split_out_lo(p):
                pool.wait_ge(owhi_done, p + 1)
                pool.tensor_tensor(ow_lo[:, :, :], ow[:, :, :], ow_hi[:, :, :].bitcast(F32),
                                   ALU.subtract).then_inc(owlo_done, 1)

            def attention(a, seg):
                for h in range(2):
                    pool.wait_ge(silu_done, 6 * a + 3 + h)
                    wait(pool, attn_done, 2 * a + h - 1)
                    decay = table[:, TAB_Q + h * P:TAB_Q + (h + 1) * P]
                    pool.tensor_tensor(qd[:, h].rearrange("p (c n) -> p c n", c=CH),
                                       q[:, h].rearrange("p (c n) -> p c n", c=CH),
                                       decay.unsqueeze(1).to_broadcast([P, CH, P]),
                                       ALU.mult).then_inc(qd_done, 1)
                for h in range(2):
                    pool.wait_ge(sq_done, 2 * a + h + 1)
                    wait(pool, ss_done, 2 * a + h)
                    pool.tensor_tensor(sumsq[:, tokens(seg)], sumsq[:, tokens(seg)], sq[:, h],
                                       ALU.add).then_inc(ss_done, 1)
                for h in range(2):
                    pool.wait_ge(ghi_done, 2 * a + h + 1)
                    pool.tensor_tensor(g_lo[:, h], g[:, h], g_hi[:, h].bitcast(F32),
                                       ALU.subtract).then_inc(glo_done, 1)

            pool.memset(ident[:, :], 0.0).then_inc(const_done, 1)
            pool.wait_ge(const_done, 1)
            pool.affine_select(out=ident[:, :], in_=ident[:, :], compare_op=ALU.not_equal, fill=1.0,
                               base=0, pattern=[[-1, P]], channel_multiplier=1).then_inc(const_done, 1)
            pool.memset(ones[:, :], 1.0).then_inc(const_done, 1)
            pool.memset(sumsq[:, :], 0.0).then_inc(ss_cleared, 1)
            for kind in range(4):
                split_lo(0, kind)
            pool.wait_ge(ss_cleared, 1)
            pool.wait_ge(table_ready, 1)
            attention(0, 0)
            split_out_lo(0)
            with pool.Fori(0, PAIRS - 1) as i:
                for j in range(NSEG):
                    a = 4 * i + 1 + j
                    if j == 3:
                        pool.wait_ge(table_ready, i + 2)
                    attention(a, (1 + j) % NSEG)
                    if j == 1:
                        for kind in range(4):
                            split_lo(i + 1, kind)
                    if j == 3:
                        split_out_lo(i + 1)
            for j in range(NSEG - 1):
                attention(STEPS - 3 + j, 1 + j)

            pool.wait_ge(part_done, 1)
            pool.partition_all_reduce(all_max[:, :], part_max[:, :], P,
                                      bass.bass_isa.ReduceOp.max).then_inc(all_max_done, 1)

            def hidden(n, par):
                for t in range(2):
                    pool.wait_ge(hhi_done, 2 * n + t + 1)
                    pool.tensor_tensor(h_lo[:, par, t], hid[:, t], h_hi[:, par, t].bitcast(F32),
                                       ALU.subtract).then_inc(hlo_done, 1)

            hidden(0, 0)
            hidden(1, 1)
            with pool.Fori(0, FG - 1) as i:
                for j in range(NSEG):
                    hidden(4 * i + 2 + j, j % 2)
            def last_residual(s):
                for t in range(CH):
                    tile = s * CH + t
                    pool.wait_ge(normed, 3 * TILES + tile + 1)
                    pool.tensor_tensor(y[:, tile], y[:, tile], y2[:, tile],
                                       ALU.add).then_inc(final_done, 1)

            hidden(FSTEPS - 2, 0)
            last_residual(0)
            hidden(FSTEPS - 1, 1)
            for s in range(1, NSEG):
                last_residual(s)

        @block.scalar
        def _(act):
            def square_root(count):
                act.wait_ge(var_ready, count + 1)
                act.activation(stdev[:, :], var_eps[:, :], ACT.Sqrt).then_inc(sd_ready, 1)

            def x_hi_part(t, psum, count):
                act.wait_ge(xt_done, count + 1)
                act.activation(x_hi[:, :, chunk(t)], psum[:, :].rearrange("p (h n) -> p h n", h=HT),
                               ACT.Copy).then_inc(xhi_done, 1)

            def split_hi(p, kind, n):
                act.wait_ge(raw_in[kind % 2], 32 * p + 16 * (kind // 2) + 16)
                if n is not None:
                    act.wait_ge(proj_done, 8 * n + (2, 4, 6, 8)[kind])
                act.activation(w_hi[:, kind], raw[:, kind % 2], ACT.Copy).then_inc(whi_done, 1)

            def split_out_hi(p, a):
                act.wait_ge(ow_scaled, 2 * p + 2)
                wait(act, yproj_done, 4 * a)
                act.activation(ow_hi[:, :, :], ow[:, :, :], ACT.Copy).then_inc(owhi_done, 1)

            def sigmoid(n, u):
                act.wait_ge(proj_done, 8 * n + u + 1)
                a = n - 1
                h = u % 2
                if u < 2:
                    wait(act, score_done, 2 * a + h + 1)
                    dst, src = k[:, h], proj_ps[h][:, :]
                elif u < 4:
                    wait(act, score_done, 2 * a + h + 1)
                    wait(act, qd_done, 2 * a + h + 1)
                    dst, src = q[:, h], proj_ps[h][:, :]
                elif u < 6:
                    wait(act, attn_done, 2 * a + 2)
                    dst = v[:, 2 * h:2 * h + 2].rearrange("p c h d -> p (c h d)")
                    src = proj_ps[h][:, :]
                else:
                    wait(act, glo_done, 2 * a + h + 1)
                    dst, src = g[:, h], proj_ps[h][:, :]
                act.activation(dst, src, ACT.Sigmoid).then_inc(sig_done, 1)

            def k_decay(a, h):
                act.wait_ge(kt_done, 2 * a + h + 1)
                wait(act, contrib_done, 2 * a + h - 1)
                act.activation(kd[:, h].rearrange("p c d -> p (c d)"), kt_at[h][:, :], ACT.Copy,
                               scale=table[:, TAB_K + h:TAB_K + h + 1]).then_inc(kd_done, 1)

            def square(a, h):
                act.wait_ge(attn_done, 2 * a + h + 1)
                wait(act, ss_done, 2 * a + h - 1)
                act.activation(sq[:, h], kt_at[h][:, :], ACT.Square).then_inc(sq_done, 1)

            def gated_hi(a, h):
                act.wait_ge(gated_done, 2 * a + h + 1)
                wait(act, yproj_done, 4 * a)
                act.activation(g_hi[:, h], g[:, h], ACT.Copy).then_inc(ghi_done, 1)

            def step(a, n, table_count=None, split=None, out_split=None):
                if table_count is not None:
                    act.wait_ge(table_ready, table_count)
                for h in range(2):
                    k_decay(a, h)
                    if n is not None:
                        sigmoid(n, h)
                if n is not None:
                    sigmoid(n, 2)
                    sigmoid(n, 3)
                square(a, 0)
                square(a, 1)
                if out_split is not None:
                    split_out_hi(out_split, a)
                gated_hi(a, 0)
                gated_hi(a, 1)
                if n is not None:
                    sigmoid(n, 4)
                    if split is not None:
                        split_hi(split, KK, n)
                    sigmoid(n, 5)
                    if split is not None:
                        split_hi(split, QQ, n)
                    sigmoid(n, 6)
                    if split is not None:
                        split_hi(split, VV, n)
                    sigmoid(n, 7)
                    if split is not None:
                        split_hi(split, GG, n)

            split_hi(0, KK, None)
            split_hi(0, QQ, None)
            square_root(0)
            for t in range(CH):
                x_hi_part(t, ln1_ring[t % 6], t)
            split_hi(0, VV, None)
            split_hi(0, GG, None)
            for s in range(1, NSEG):
                square_root(s)
            for u in range(8):
                sigmoid(0, u)
                for t in range(CH + 2 * u, min(CH + 2 * u + 2, TILES)):
                    x_hi_part(t, ln1_ring[t % 6], t)
            def four_steps(i, checks):
                for j in range(NSEG):
                    a = 4 * i + 1 + j
                    if checks and j < CHECKS_PER_PAIR:
                        c = CHECKS_PER_PAIR * i + j
                        act.wait_ge(block_done, c)
                        act.dma_start(check[:, :], w_blocks[c]).then_inc(check_in, 16)
                    step(a, a + 1, table_count=i + 2 if j == 3 else None,
                         split=i + 1 if j == 1 else None, out_split=i + 1 if j == 3 else None)

            step(0, 1, table_count=1, out_split=0)
            with act.Fori(0, CHECK_PAIRS) as i:
                four_steps(i, True)
            with act.Fori(CHECK_PAIRS, PAIRS - 1) as i:
                four_steps(i, False)
            step(STEPS - 3, STEPS - 2)
            step(STEPS - 2, STEPS - 1)
            step(STEPS - 1, None)

            def ffn_split_hi(n, t, m):
                act.wait_ge(fraw_in, 16 * (n + 1))
                if m is not None:
                    act.wait_ge(fproj_done, 4 * m + 2 * t + 2)
                act.activation(f_hi[:, t], fraw[:, t], ACT.Copy).then_inc(fhi_done, 1)

            def down_split_hi(n, d):
                act.wait_ge(draw_in, 16 * (n + 1))
                wait(act, down_done, 4 * d)
                act.activation(d_hi[:, :, :], draw[:, :, :], ACT.Copy).then_inc(dhi_done, 1)

            def ffn_sigmoid(m, t):
                act.wait_ge(fproj_done, 4 * m + 2 * t + 1)
                wait(act, hlo_done, 2 * m + t - 1)
                act.activation(hid[:, t], ffn_ps[2 * t][:, :], ACT.Sigmoid,
                               scale=fs[:, t:t + 1]).then_inc(fsig_done, 1)

            def hidden_hi(m, par, t):
                act.wait_ge(hid_done, 2 * m + t + 1)
                wait(act, down_done, 4 * (m - 1))
                act.activation(h_hi[:, par, t], hid[:, t], ACT.Copy).then_inc(hhi_done, 1)

            def ffn_step(m, par, scales=None, split=None, down=None):
                if scales is not None:
                    act.wait_ge(fs_ready, scales)
                if down is not None:
                    down_split_hi(down, m - 1)
                for t in range(2):
                    ffn_sigmoid(m, t)
                    hidden_hi(m, par, t)
                    if split is not None:
                        ffn_split_hi(split, t, m)

            def mid_norm(s):
                square_root(NSEG + 2 * s)
                square_root(NSEG + 2 * s + 1)
                for t in range(CH):
                    x_hi_part(s * CH + t, sc_st[t % 2], TILES + s * CH + t)

            act.wait_ge(yacc_done, 4 * STEPS)
            act.wait_ge(ss_done, 2 * STEPS)
            ffn_split_hi(0, 0, None)
            ffn_split_hi(0, 1, None)
            mid_norm(0)
            ffn_step(0, 0, scales=1)
            mid_norm(1)
            ffn_step(1, 1, down=0)
            mid_norm(2)
            mid_norm(3)
            with act.Fori(0, FG - 1) as i:
                for j in range(NSEG):
                    ffn_step(4 * i + 2 + j, j % 2, scales=i + 2 if j == 2 else None,
                             split=i + 1 if j == 1 else None, down=i + 1 if j == 3 else None)
            square_root(3 * NSEG)
            ffn_step(FSTEPS - 2, 0)
            square_root(3 * NSEG + 1)
            ffn_step(FSTEPS - 1, 1)
            square_root(3 * NSEG + 2)
            square_root(3 * NSEG + 3)

        @block.vector
        def _(dve):
            own = [0]

            def norm_statistics(src, extra=None):
                for t in range(CH):
                    dve.bn_stats(stats[:, t], src(t)).then_inc(ln_own, 1)
                own[0] += CH
                dve.wait_ge(ln_own, own[0])
                for t in range(CH):
                    dve.bn_aggr(meanvar[:, t], stats[:, t]).then_inc(ln_own, 1)
                own[0] += CH
                dve.wait_ge(ln_own, own[0])
                if extra is None:
                    dve.tensor_scalar(var_eps[:, :], meanvar[:, :, 1], LN_EPS, None,
                                      ALU.add).then_inc(var_ready, 1)
                else:
                    dve.tensor_tensor(var_eps[:, :], meanvar[:, :, 1], extra,
                                      ALU.add).then_inc(var_ready, 1)

            def normalise(src, dst, number):
                dve.wait_ge(sd_ready, number + 1)
                dve.reciprocal(rstd[:, :], stdev[:, :]).then_inc(ln_own, 1)
                own[0] += 1
                dve.wait_ge(ln_own, own[0])
                for t in range(CH):
                    dve.tensor_scalar(dst(t), src(t), meanvar[:, t, 0:1], rstd[:, t:t + 1],
                                      ALU.subtract, ALU.mult).then_inc(normed, 1)

            def layer_norm(src, dst, number, extra=None):
                norm_statistics(src, extra)
                normalise(src, dst, number)

            def x_lo_part(t, psum, count):
                dve.wait_ge(xhi_done, count + 1)
                dve.tensor_tensor(x_lo[:, :, chunk(t)], psum[:, :].rearrange("p (h n) -> p h n", h=HT),
                                  x_hi[:, :, chunk(t)].bitcast(F32), ALU.subtract).then_inc(xlo_done, 1)

            def next_table(a, p):
                wait(dve, kd_done, 2 * a)
                wait(dve, qd_done, 2 * a)
                dve.wait_ge(table_in, 16 * (p + 1))
                dve.tensor_copy(table[:, :], table_stage[:, :]).then_inc(table_ready, 1)
                dve.wait_ge(table_ready, p + 1)

            def scale_out_weights(p):
                dve.wait_ge(ow_in, 16 * (p + 1))
                dve.wait_ge(norm_in, 16 * (p + 1))
                for h in range(2):
                    dve.tensor_scalar(ow[:, h], ow[:, h], nw[:, h:h + 1], None,
                                      ALU.mult).then_inc(ow_scaled, 1)

            def silu(n, u):
                dve.wait_ge(sig_done, 8 * n + u + 1)
                h = u % 2
                dst = (k[:, h], q[:, h], v[:, 2 * h:2 * h + 2].rearrange("p c h d -> p (c h d)"))[u // 2]
                dve.tensor_tensor(dst, proj_ps[h][:, :], dst, ALU.mult).then_inc(silu_done, 1)

            def decay_scores(a, h):
                dve.wait_ge(score_done, 2 * a + h + 1)
                wait(dve, attn_done, 2 * a + h - 1)
                mask = table[:, TAB_D + h * P:TAB_D + (h + 1) * P]
                dve.tensor_tensor(pd[:, h], sc_st[h][:, :].rearrange("p (c n) -> p c n", c=CH),
                                  mask.unsqueeze(1).to_broadcast([P, CH, P]),
                                  ALU.mult).then_inc(pdec_done, 1)

            def update_state(a, odd, h):
                dve.wait_ge(contrib_done, 2 * a + h + 1)
                done = states_before(a, odd) + h * (CH - odd)
                for c in range(CH - odd):
                    new = sc_st[h][:, chunk(c)]
                    if c == 0 and not odd:
                        dve.tensor_copy(state[:, h, 0], new).then_inc(state_done, 1)
                        continue
                    wait(dve, state_done, done + c)
                    dve.scalar_tensor_tensor(state[:, h, c], state[:, h, (c - 1) % CH],
                                             table[:, TAB_B + h:TAB_B + h + 1], new,
                                             ALU.mult, ALU.add).then_inc(state_done, 1)

            def gate(a, h):
                dve.wait_ge(sq_done, 2 * a + h + 1)
                dve.wait_ge(sig_done, 8 * a + 7 + h)
                dve.tensor_tensor(g[:, h], kt_at[h][:, :], g[:, h], ALU.mult).then_inc(gated_done, 1)

            def add_out(a, seg, t):
                dve.wait_ge(yproj_done, 4 * a + t + 1)
                tile = y[:, seg * CH + t]
                dve.tensor_tensor(tile, yp[t % 2][:, :], tile, ALU.add).then_inc(yacc_done, 1)

            def step(a, seg, n, pair=None):
                odd = seg % 2
                if pair is not None:
                    next_table(a, pair)
                for h in range(2):
                    decay_scores(a, h)
                    if n is not None:
                        silu(n, h)
                update_state(a, odd, 0)
                update_state(a, odd, 1)
                if n is not None:
                    silu(n, 2)
                    silu(n, 3)
                if pair is not None:
                    scale_out_weights(pair)
                gate(a, 0)
                gate(a, 1)
                if n is not None:
                    silu(n, 4)
                    silu(n, 5)
                for t in range(CH):
                    add_out(a, seg, t)

            for s in range(NSEG):
                dve.wait_ge(x_in[s], 16)
                layer_norm(lambda t: y[:, s * CH + t], lambda t: y[:, s * CH + t], s)
                if s == 0:
                    for t in range(CH):
                        x_lo_part(t, ln1_ring[t % 6], t)
            for u in range(8):
                if u < 6:
                    silu(0, u)
                for t in range(CH + 2 * u, min(CH + 2 * u + 2, TILES)):
                    x_lo_part(t, ln1_ring[t % 6], t)
            dve.wait_ge(xt_done, TILES)
            dve.memset(y[:, :, :].rearrange("p t h -> p (t h)"), 0.0).then_inc(y_cleared, 1)
            dve.wait_ge(y_cleared, 1)
            def look_at_block(c, j):
                dve.wait_ge(check_in, 16 * (c + 1))
                dve.wait_ge(max_done, c)
                dve.tensor_reduce(block_max[:, j:j + 1], check[:, :], AX.X, ALU.max,
                                  apply_absolute_value=True).then_inc(block_done, 1)
                dve.wait_ge(block_done, c + 1)
                dve.tensor_tensor(ints_max[:, j:j + 1], ints_max[:, j:j + 1], block_max[:, j:j + 1],
                                  ALU.max).then_inc(max_done, 1)

            def four_steps(i, checks):
                for j in range(NSEG):
                    a = 4 * i + 1 + j
                    step(a, (1 + j) % NSEG, a + 1, pair=i + 1 if j == 3 else None)
                    if checks and j < CHECKS_PER_PAIR:
                        look_at_block(CHECKS_PER_PAIR * i + j, j)

            dve.memset(ints_max[:, :], 0.0).then_inc(max_cleared, 1)
            step(0, 0, 1, pair=0)
            dve.wait_ge(max_cleared, 1)
            with dve.Fori(0, CHECK_PAIRS) as i:
                four_steps(i, True)
            dve.wait_ge(max_done, WIDTH_CHECKS)
            dve.tensor_reduce(part_max[:, :], ints_max[:, :], AX.X, ALU.max).then_inc(part_done, 1)
            with dve.Fori(CHECK_PAIRS, PAIRS - 1) as i:
                four_steps(i, False)
            step(STEPS - 3, 1, STEPS - 2)
            step(STEPS - 2, 2, STEPS - 1)
            step(STEPS - 1, 3, None)

            def new_scales(n):
                dve.wait_ge(fs_in, 16 * (n + 1))
                dve.tensor_copy(fs[:, :], fs_stage[:, :]).then_inc(fs_ready, 1)
                dve.wait_ge(fs_ready, n + 1)

            def ffn_split_lo(n, t):
                dve.wait_ge(fhi_done, 2 * n + t + 1)
                dve.tensor_tensor(f_lo[:, t], fraw[:, t], f_hi[:, t].bitcast(F32),
                                  ALU.subtract).then_inc(flo_done, 1)

            def down_split_lo(n):
                dve.wait_ge(dhi_done, n + 1)
                dve.tensor_tensor(d_lo[:, :, :], draw[:, :, :], d_hi[:, :, :].bitcast(F32),
                                  ALU.subtract).then_inc(dlo_done, 1)

            def hidden(m, t):
                dve.wait_ge(fsig_done, 2 * m + t + 1)
                dve.scalar_tensor_tensor(hid[:, t], ffn_ps[2 * t][:, :], fs[:, t:t + 1], hid[:, t],
                                         ALU.mult, ALU.mult).then_inc(fgate_done, 1)
                dve.wait_ge(fproj_done, 4 * m + 2 * t + 2)
                dve.wait_ge(fgate_done, 2 * m + t + 1)
                dve.scalar_tensor_tensor(hid[:, t], ffn_ps[2 * t + 1][:, :], fs[:, 2 + t:3 + t],
                                         hid[:, t], ALU.mult, ALU.mult).then_inc(hid_done, 1)

            def add_down(d, seg, t):
                dve.wait_ge(down_done, 4 * d + t + 1)
                tile = y2[:, seg * CH + t]
                dve.tensor_tensor(tile, yp[t % 2][:, :], tile, ALU.add).then_inc(y2acc_done, 1)

            def ffn_step(m, d, seg, scales=None, split=None, down=None):
                if scales is not None:
                    new_scales(scales)
                if down is not None:
                    down_split_lo(down)
                for t in range(2):
                    if m is not None:
                        hidden(m, t)
                        if split is not None:
                            ffn_split_lo(split, t)
                    if d is not None:
                        add_down(d, seg, 2 * t)
                        add_down(d, seg, 2 * t + 1)

            def mid_norm(s):
                def tile(t):
                    return y[:, s * CH + t]

                layer_norm(tile, tile, NSEG + 2 * s, extra=rms_term[:, s * CH:(s + 1) * CH])
                dve.wait_ge(normed, TILES + 2 * CH * s + CH)
                dve.wait_ge(xres_in, 16 * (s + 1))
                seg = y[:, s * CH:(s + 1) * CH].rearrange("p t h -> p (t h)")
                dve.tensor_tensor(seg, seg, xres[:, :, :].rearrange("p t h -> p (t h)"),
                                  ALU.add).then_inc(ln_own, 1)
                own[0] += 1
                dve.wait_ge(ln_own, own[0])
                wait(dve, xt_done, TILES + CH * s)
                layer_norm(tile, lambda t: xn[:, t], NSEG + 2 * s + 1)
                for t in range(CH):
                    x_lo_part(s * CH + t, sc_st[t % 2], TILES + s * CH + t)

            def final_norm_a(s):
                dve.wait_ge(y2acc_done, NSEG * CH * (FG - 1) + CH * (s + 1))
                for t in range(CH):
                    dve.tensor_tensor(y2[:, s * CH + t], y2[:, s * CH + t], ds[:, :],
                                      ALU.mult).then_inc(ln_own, 1)
                own[0] += CH
                dve.wait_ge(ln_own, own[0])
                norm_statistics(lambda t: y2[:, s * CH + t])

            def final_norm_b(s):
                normalise(lambda t: y2[:, s * CH + t], lambda t: y2[:, s * CH + t], 3 * NSEG + s)

            dve.wait_ge(all_max_done, 1)
            dve.tensor_scalar(wide[:, :], all_max[:, :], F32R_EXACT, None,
                              ALU.is_gt).then_inc(wide_ready, 1)
            dve.wait_ge(glo_done, 2 * STEPS)
            dve.memset(y2[:, 0:TILES - CH].rearrange("p t h -> p (t h)"), 0.0).then_inc(y2_cleared, 1)
            dve.wait_ge(ssum_done, 1)
            dve.tensor_scalar(rms_term[:, :], sc_st[0][:, 0:TILES], LN_EPS / (HEADS * HD),
                              LN_EPS * RMS_EPS, ALU.mult, ALU.add).then_inc(ln_own, 1)
            own[0] += 1
            dve.wait_ge(ln_own, own[0])
            ffn_split_lo(0, 0)
            ffn_split_lo(0, 1)
            mid_norm(0)
            new_scales(0)
            ffn_step(0, None, None)
            dve.wait_ge(y2_cleared, 1)
            mid_norm(1)
            ffn_step(1, 0, 0, down=0)
            mid_norm(2)
            mid_norm(3)
            dve.wait_ge(xt_done, 2 * TILES)
            dve.memset(xn.rearrange("p t h -> p (t h)"), 0.0).then_inc(y2_cleared, 1)
            dve.wait_ge(y2_cleared, 2)
            with dve.Fori(0, FG - 1) as i:
                for j in range(NSEG):
                    m = 4 * i + 2 + j
                    ffn_step(m, m - 1, (1 + j) % NSEG, scales=i + 1 if j == 2 else None,
                             split=i + 1 if j == 1 else None, down=i + 1 if j == 3 else None)
            dve.wait_ge(ds_in, 16)
            final_norm_a(0)
            ffn_step(FSTEPS - 2, FSTEPS - 3, 1)
            final_norm_b(0)
            final_norm_a(1)
            ffn_step(FSTEPS - 1, FSTEPS - 2, 2)
            final_norm_b(1)
            final_norm_a(2)
            final_norm_b(2)
            ffn_step(None, FSTEPS - 1, 3)
            final_norm_a(3)
            final_norm_b(3)

        @block.tensor
        def _(pe):
            def split_product(psum, stationary, moving, done=None, drop=None):
                terms = []
                for s, m in zip(stationary, moving):
                    terms.append((s[0], m[0]))
                    if drop != "moving":
                        terms.append((s[0], m[1]))
                    if drop != "stationary":
                        terms.append((s[1], m[0]))
                for n, (s, m) in enumerate(terms):
                    last = pe.matmul(psum, s, m, start=n == 0, stop=n == len(terms) - 1)
                if done is not None:
                    last.then_inc(done, 1)

            def transpose_x(t, src, psum, count):
                pe.wait_ge(normed, count)
                for h in range(HT):
                    last = pe.transpose(psum[:, chunk(h)], src[:, chunk(h)], ident[:, :])
                last.then_inc(xt_done, 1)

            def unit(n, seg, u, new_pair=None):
                if new_pair is not None and u in (0, 2, 4, 6):
                    pe.wait_ge(wlo_done, 4 * new_pair + u // 2 + 1)
                if u < 2:
                    wait(pe, sig_done, 8 * n - 1 + u)
                else:
                    pe.wait_ge(silu_done, 6 * n + u - 1)
                h = u % 2
                if u in (4, 5):
                    for c in range(2):
                        tok = slice(seg * SEG + (2 * h + c) * P, seg * SEG + (2 * h + c + 1) * P)
                        split_product(
                            proj_ps[h][:, c * 2 * HD:(c + 1) * 2 * HD],
                            [(x_hi[:, r, tok], x_lo[:, r, tok]) for r in range(HT)],
                            [(w_hi[:, VV, r].rearrange("p h d -> p (h d)"),
                              w_lo[:, VV, r].rearrange("p h d -> p (h d)")) for r in range(HT)],
                            proj_done if c == 1 else None)
                    return
                kind = (KK, QQ, VV, GG)[u // 2]
                split_product(proj_ps[h][:, :],
                              [(w_hi[:, kind, r, h], w_lo[:, kind, r, h]) for r in range(HT)],
                              [(x_hi[:, r, tokens(seg)], x_lo[:, r, tokens(seg)]) for r in range(HT)],
                              proj_done)

            def transposes_and_scores(a, h):
                pe.wait_ge(silu_done, 6 * a + 3 + h)
                wait(pe, gated_done, 2 * a + h - 1)
                for c in range(CH):
                    last = pe.transpose(kt_at[h][:, chunk(c)], k[:, h, chunk(c)], ident[:, :])
                last.then_inc(kt_done, 1)
                for c in range(CH):
                    last = pe.matmul(sc_st[h][:, chunk(c)], k[:, h, chunk(c)], q[:, h, chunk(c)],
                                     start=True, stop=True)
                last.then_inc(score_done, 1)

            def contributions(a, odd, h):
                pe.wait_ge(silu_done, 6 * a + 6)
                pe.wait_ge(kd_done, 2 * a + h + 1)
                pe.wait_ge(pdec_done, 2 * a + h + 1)
                for c in range(CH - odd):
                    last = pe.matmul(sc_st[h][:, chunk(c)], kd[:, h, c], v[:, c, h],
                                     start=True, stop=True)
                last.then_inc(contrib_done, 1)

            def attend(a, odd, h):
                pe.wait_ge(qd_done, 2 * a + h + 1)
                pe.wait_ge(state_done, states_before(a, odd) + (h + 1) * (CH - odd))
                for c in range(CH):
                    inter = c > 0 or odd
                    last = pe.matmul(kt_at[h][:, chunk(c)], v[:, c, h], pd[:, h, c],
                                     start=True, stop=not inter)
                    if inter:
                        last = pe.matmul(kt_at[h][:, chunk(c)], state[:, h, (c - 1) % CH],
                                         qd[:, h, chunk(c)], start=False, stop=True)
                last.then_inc(attn_done, 1)

            def project_out(a, t, new_pair=None):
                if t == 0:
                    pe.wait_ge(glo_done, 2 * a + 2)
                    if new_pair is not None:
                        pe.wait_ge(owlo_done, new_pair + 1)
                wait(pe, yacc_done, 4 * a + t - 1)
                split_product(yp[t % 2][:, :],
                              [(g_hi[:, h, chunk(t)], g_lo[:, h, chunk(t)]) for h in range(2)],
                              [(ow_hi[:, h], ow_lo[:, h]) for h in range(2)],
                              yproj_done)

            def step(a, seg, n, pair_n=None, pair_a=None):
                odd = seg % 2
                seg_n = (seg + 1) % NSEG

                def next_unit(u):
                    if n is not None:
                        unit(n, seg_n, u, pair_n)

                transposes_and_scores(a, 0)
                next_unit(0)
                transposes_and_scores(a, 1)
                next_unit(1)
                contributions(a, odd, 0)
                contributions(a, odd, 1)
                next_unit(2)
                next_unit(3)
                attend(a, odd, 0)
                attend(a, odd, 1)
                next_unit(4)
                next_unit(5)
                next_unit(6)
                project_out(a, 0, pair_a)
                project_out(a, 1)
                next_unit(7)
                project_out(a, 2)
                project_out(a, 3)

            pe.wait_ge(const_done, 3)
            for t in range(CH):
                transpose_x(t, y[:, t], ln1_ring[t], t + 1)
            pe.wait_ge(xlo_done, CH)
            for u in range(8):
                unit(0, 0, u, 0)
                for t in range(CH + 2 * u, min(CH + 2 * u + 2, TILES)):
                    wait(pe, xlo_done, t - 5)
                    transpose_x(t, y[:, t], ln1_ring[t % 6], t + 1)
            pe.wait_ge(xlo_done, TILES)
            step(0, 0, 1, pair_a=0)
            with pe.Fori(0, PAIRS - 1) as i:
                for j in range(NSEG):
                    a = 4 * i + 1 + j
                    step(a, (1 + j) % NSEG, a + 1, pair_n=i + 1 if j == 2 else None,
                         pair_a=i + 1 if j == 3 else None)
            step(STEPS - 3, 1, STEPS - 2)
            step(STEPS - 2, 2, STEPS - 1)
            step(STEPS - 1, 3, None)

            def ffn_unit(narrow, m, seg, u, new_group=None):
                t, up = u // 2, u % 2
                if new_group is not None and up == 0:
                    pe.wait_ge(flo_done, 2 * new_group + t + 1)
                wait(pe, hid_done, 2 * (m - 1) + t + 1)
                split_product(ffn_ps[u][:, :],
                              [(f_hi[:, t, up, r], f_lo[:, t, up, r]) for r in range(HT)],
                              [(x_hi[:, r, tokens(seg)], x_lo[:, r, tokens(seg)]) for r in range(HT)],
                              fproj_done, "stationary" if narrow else None)

            def project_down(narrow, d, par, t, new_group=None):
                if t == 0:
                    pe.wait_ge(hlo_done, 2 * d + 2)
                    if new_group is not None:
                        pe.wait_ge(dlo_done, new_group + 1)
                if isinstance(d, int) and d == 0:
                    pe.wait_ge(yacc_done, 4 * STEPS)
                wait(pe, y2acc_done, 4 * d + t - 1)
                split_product(yp[t % 2][:, :],
                              [(h_hi[:, par, f, chunk(t)], h_lo[:, par, f, chunk(t)]) for f in range(2)],
                              [(d_hi[:, f], d_lo[:, f]) for f in range(2)],
                              down_done, "moving" if narrow else None)

            def ffn_step(narrow, m, seg, d, par, new_group=None, down_group=None):
                for t in range(2):
                    if m is not None:
                        ffn_unit(narrow, m, seg, 2 * t, new_group)
                        ffn_unit(narrow, m, seg, 2 * t + 1, new_group)
                    if d is not None:
                        project_down(narrow, d, par, 2 * t, down_group)
                        project_down(narrow, d, par, 2 * t + 1)

            def mid_transposes(s):
                for t in range(CH):
                    count = TILES + s * CH + t
                    wait(pe, xlo_done, count - 1)
                    transpose_x(s * CH + t, xn[:, t], sc_st[t % 2],
                                TILES + 2 * CH * s + CH + t + 1)

            pe.wait_ge(ss_done, 2 * STEPS)
            pe.wait_ge(state_done, states_before(STEPS, False))
            for t in range(TILES):
                last = pe.matmul(sc_st[0][:, t:t + 1], sumsq[:, chunk(t)], ones[:, :],
                                 start=True, stop=True)
            last.then_inc(ssum_done, 1)
            pe.wait_ge(gated_done, 2 * STEPS)
            mid_transposes(0)
            pe.wait_ge(xlo_done, TILES + CH)
            def ffn_half(narrow):
                ffn_step(narrow, 0, 0, None, None, new_group=0)
                mid_transposes(1)
                pe.wait_ge(xlo_done, TILES + 2 * CH)
                ffn_step(narrow, 1, 1, 0, 0, down_group=0)
                mid_transposes(2)
                mid_transposes(3)
                pe.wait_ge(xlo_done, 2 * TILES)
                with pe.Fori(0, FG - 1) as i:
                    for j in range(NSEG):
                        m = 4 * i + 2 + j
                        ffn_step(narrow, m, (2 + j) % NSEG, m - 1, (1 + j) % 2,
                                 new_group=i + 1 if j == 2 else None,
                                 down_group=i + 1 if j == 3 else None)
                ffn_step(narrow, FSTEPS - 2, 2, FSTEPS - 3, 1)
                ffn_step(narrow, FSTEPS - 1, 3, FSTEPS - 2, 0)
                ffn_step(narrow, None, None, FSTEPS - 1, 1)

            pe.wait_ge(wide_ready, 1)
            needs_lo = pe.value_load(wide[0:1, 0:1], min_val=0, max_val=1)
            with pe.If(needs_lo == 1):
                ffn_half(False)
            with pe.Else():
                ffn_half(True)


def decay_tables(np):
    layer, layers = 1, 32
    base = np.float32(1.0 / 2.0 ** (8.0 / HEADS))
    factor = np.float32(1.0 - layer / (layers - 1 + 1e-05) + 1e-05)
    slope = (base ** (np.arange(HEADS, dtype=np.float32) + np.float32(1)) * factor).astype(np.float32)
    r = np.arange(P, dtype=np.float32) + np.float32(1)
    t = np.zeros((PAIRS, P, TAB), np.float32)
    for head in range(HEADS):
        p, h, s = head // 2, head % 2, slope[head]
        diff = r[None, :] - r[:, None]
        t[p, :, TAB_D + h * P:TAB_D + (h + 1) * P] = np.where(diff >= 0, np.exp(-s * np.abs(diff)), 0)
        t[p, :, TAB_Q + h * P:TAB_Q + (h + 1) * P] = np.exp(-s * r)[None, :]
        t[p, :, TAB_K + h] = np.exp(-s * (np.float32(P) - r))
        t[p, :, TAB_B + h] = np.exp(-s * np.float32(P))
    return t


def kernel(L0_attn_hidden_states, L0_attn_qkv_w, L0_attn_out_w, L0_attn_gate_w, L0_attn_norm_w,
           L0_ffn_gate_t, L0_ffn_up_t, L0_ffn_down_t, L0_ffn_gate_s, L0_ffn_up_s, L0_ffn_down_s):
    import numpy as np
    import concourse.bacc as bacc
    from concourse.bass_utils import run_bass_kernel_spmd

    qkv = np.asarray(L0_attn_qkv_w).reshape(PAIRS, 2, 3, HD, HT, P)
    gate = np.asarray(L0_attn_gate_w).reshape(PAIRS, 2, 1, HD, HT, P)
    w = np.concatenate([qkv[:, :, 1:2], qkv[:, :, 0:1], qkv[:, :, 2:3], gate], axis=2)
    w_attn = w.transpose(0, 2, 5, 4, 1, 3)
    w_out = np.asarray(L0_attn_out_w).reshape(HID, PAIRS, 2, HD).transpose(1, 3, 2, 0)
    norm_w = np.asarray(L0_attn_norm_w).reshape(PAIRS, 2, HD).transpose(0, 2, 1)
    gu = np.stack([np.asarray(L0_ffn_gate_t), np.asarray(L0_ffn_up_t)]).reshape(2, FG, 2, P, HT, P)
    w_ffn = gu.transpose(1, 5, 2, 0, 4, 3)
    w_down = np.asarray(L0_ffn_down_t).reshape(HID, FG, 2, P).transpose(1, 3, 2, 0)
    scales = np.stack([np.asarray(L0_ffn_gate_s), np.asarray(L0_ffn_up_s)]).reshape(2, FG, 2, P)
    arrays = {
        "x": np.asarray(L0_attn_hidden_states).reshape(TOK, HID),
        "w_attn": w_attn, "w_out": w_out, "norm_w": norm_w, "tables": decay_tables(np),
        "w_ints": np.concatenate([w_ffn.ravel(), w_down.ravel()]),
        "ffn_scales": scales.transpose(1, 3, 0, 2).reshape(FG, P, 4),
        "down_s": np.asarray(L0_ffn_down_s),
    }
    arrays = {name: np.ascontiguousarray(a) for name, a in arrays.items()}
    nc = bacc.Bacc("TRN2", target_bir_lowering=False, num_devices=1)
    aps = [nc.dram_tensor(name, a.shape, mybir.dt.from_np(a.dtype), kind="ExternalInput").ap()
           for name, a in arrays.items()]
    out = nc.dram_tensor("out", (TOK, HID), F32, kind="ExternalOutput").ap()
    sandwich_kernel(nc, *aps, out)
    result = run_bass_kernel_spmd(nc, [arrays], core_ids=[0])
    return result.results[0]["out"].reshape(BATCH, SEQ, HID)
```

```python
from contextlib import ExitStack

import concourse.bass as bass
from concourse import mybir
from concourse.alu_op_type import AluOpType as ALU

P = 128
BATCH, SEQ, HID = 2, 1024, 512
TOK = BATCH * SEQ
HEADS, HD = 32, 128
FF = 1792
LN_EPS = 1e-5
RMS_EPS = 1e-5

SEG = 512
NSEG = TOK // SEG
SEGS_PER_BATCH = SEQ // SEG
CH = SEG // P
TILES = TOK // P
HT = HID // P
PAIRS = HEADS // 2
STEPS = PAIRS * NSEG
KK, QQ, VV, GG = range(4)
TAB_D, TAB_Q, TAB_K, TAB_B = 0, 2 * P, 4 * P, 4 * P + 2
TAB = 4 * P + 4

FG = FF // (2 * P)
FSTEPS = FG * NSEG
GU_INTS = 2 * FF * HID
WIDTH_CHECKS = 3 * FF * HID // (P * HID)
CHECKS_PER_PAIR = 3
CHECK_PAIRS = WIDTH_CHECKS // CHECKS_PER_PAIR
F32R_EXACT = 2.0 ** 12

ACT = mybir.ActivationFunctionType
AX = mybir.AxisListType
F32 = mybir.dt.float32
F32R = mybir.dt.float32r
I32 = mybir.dt.int32


def wait(eng, sem, value):
    if isinstance(value, int) and value <= 0:
        return
    eng.wait_ge(sem, value)


def states_before(a, odd):
    return 7 * a + (1 if odd else 0)


def sandwich_kernel(nc, x, w_attn, w_out, norm_w, tables, w_ints, ffn_scales, down_s, out):
    ctx = ExitStack()
    with ctx:
        def sem(name):
            return ctx.enter_context(nc.semaphore(name))

        def sb(name, shape, dt=F32, scope=ctx):
            return scope.enter_context(nc.sbuf_tensor(name, shape, dt))

        x_hi = sb("x_hi", [P, HT, TOK], F32R)
        x_lo = sb("x_lo", [P, HT, TOK], F32R)
        y = sb("y", [P, TILES, HID])
        ident = sb("ident", [P, P])
        ones = sb("ones", [P, 1])
        stats = sb("stats", [P, 4, CH, 6])
        meanvar = sb("meanvar", [P, 4, CH, 2])
        var_eps = sb("var_eps", [P, 4, CH])
        stdev = sb("stdev", [P, 4, CH])
        rstd = sb("rstd", [P, 4, CH])
        shift = sb("shift", [P, 4, CH])
        rms_term = sb("rms_term", [P, TILES])
        block_max = sb("block_max", [P, CHECKS_PER_PAIR])
        ints_max = sb("ints_max", [P, CHECKS_PER_PAIR])
        part_max = sb("part_max", [P, 1])
        all_max = sb("all_max", [P, 1])
        wide = sb("wide", [P, 1], I32)
        nw = sb("nw", [P, 2])
        table = sb("table", [P, TAB])
        fs_stage = sb("fs_stage", [P, 4])
        fs = sb("fs", [P, 4])

        def bank(name):
            return ctx.enter_context(nc.psum_tensor(name, [P, SEG], F32))

        proj_ps = [bank("proj_ps0"), bank("proj_ps1")]
        kt_at = [bank("kt_at0"), bank("kt_at1")]
        sc_st = [bank("sc_st0"), bank("sc_st1")]
        yp = [bank("yp0"), bank("yp1")]
        ln1_ring = kt_at + sc_st + yp

        x_in = [sem(f"x_in{s}") for s in range(NSEG)]
        x_first_in = [sem(f"x_first_in{t}") for t in range(CH)]
        raw_in = [sem("raw_in0"), sem("raw_in1")]
        table_in, ow_in, norm_in = sem("table_in"), sem("ow_in"), sem("norm_in")
        const_done = sem("const_done")
        ln_own = sem("ln_own")
        var_ready = sem("var_ready")
        sd_ready = sem("sd_ready")
        scale_ready = sem("scale_ready")
        normed = sem("normed")
        xt_done = sem("xt_done")
        xhi_done = sem("xhi_done")
        xlo_done = sem("xlo_done")
        y_cleared = sem("y_cleared")
        ss_cleared = sem("ss_cleared")
        whi_done, wlo_done = sem("whi_done"), sem("wlo_done")
        ow_scaled, owhi_done, owlo_done = sem("ow_scaled"), sem("owhi_done"), sem("owlo_done")
        table_ready = sem("table_ready")
        proj_done = sem("proj_done")
        kt_done = sem("kt_done")
        score_done = sem("score_done")
        contrib_done = sem("contrib_done")
        attn_done = sem("attn_done")
        yproj_done = sem("yproj_done")
        sig_done = sem("sig_done")
        kd_done = sem("kd_done")
        sq_done = sem("sq_done")
        ghi_done = sem("ghi_done")
        silu_done = sem("silu_done")
        pdec_done = sem("pdec_done")
        state_done = sem("state_done")
        gated_done = sem("gated_done")
        yacc_done = sem("yacc_done")
        qd_done = sem("qd_done")
        ss_done = sem("ss_done")
        glo_done = sem("glo_done")
        check_in = sem("check_in")
        max_cleared = sem("max_cleared")
        block_done = sem("block_done")
        max_done = sem("max_done")
        part_done = sem("part_done")
        all_max_done = sem("all_max_done")
        wide_ready = sem("wide_ready")
        ssum_done = sem("ssum_done")
        rms_ready = sem("rms_ready")
        xres_in = [sem("xres_in0"), sem("xres_in1")]
        mid_added = sem("mid_added")
        ds_in = sem("ds_in")
        fraw_in, draw_in, fs_in = sem("fraw_in"), sem("draw_in"), sem("fs_in")
        fs_ready = sem("fs_ready")
        fhi_done, fcv_done, flo_done = sem("fhi_done"), sem("fcv_done"), sem("flo_done")
        dhi_done, dcv_done, dlo_done = sem("dhi_done"), sem("dcv_done"), sem("dlo_done")
        fproj_done = sem("fproj_done")
        fsig_done = sem("fsig_done")
        fgate_done = sem("fgate_done")
        hid_done = sem("hid_done")
        hhi_done, hlo_done = sem("hhi_done"), sem("hlo_done")
        down_done = sem("down_done")
        y2_cleared = sem("y2_cleared")
        y2acc_done = sem("y2acc_done")
        x_last_in = sem("x_last_in")
        final_done = sem("final_done")
        last_done = sem("last_done")
        out_sent = sem("out_sent")

        two = ExitStack()
        raw = sb("raw", [P, 2, HT, 2, P], scope=two)
        w_hi = sb("w_hi", [P, 4, HT, 2, P], F32R, two)
        w_lo = sb("w_lo", [P, 4, HT, 2, P], F32R, two)
        ow = sb("ow", [P, 2, HID], scope=two)
        check = sb("check", [P, HID], I32, two)
        table_stage = sb("table_stage", [P, TAB], scope=two)
        k = sb("k", [P, 2, SEG], scope=two)
        q = sb("q", [P, 2, SEG], scope=two)
        qd = sb("qd", [P, 2, SEG], scope=two)
        g = sb("g", [P, 2, SEG], scope=two)
        v = sb("v", [P, CH, 2, HD], scope=two)
        kd = sb("kd", [P, 2, CH, HD], scope=two)
        pd = sb("pd", [P, 2, CH, P], scope=two)
        state = sb("state", [P, 2, CH, HD], scope=two)
        g_hi = sb("g_hi", [P, 2, SEG], F32R, two)
        g_lo = sb("g_lo", [P, 2, SEG], F32R, two)
        ow_hi = sb("ow_hi", [P, 2, HID], F32R, two)
        ow_lo = sb("ow_lo", [P, 2, HID], F32R, two)
        sq = sb("sq", [P, 2, SEG], scope=two)
        sumsq = sb("sumsq", [P, TOK], scope=two)
        two.close()

        three = ExitStack()
        fraw = sb("fraw", [P, 2, 2, HT, P], I32, three)
        f_hi = sb("f_hi", [P, 2, 2, HT, P], F32R, three)
        d_hi = sb("d_hi", [P, 2, HID], F32R, three)
        draw = sb("draw", [P, 2, HID], I32, three)
        f_lo = sb("f_lo", [P, 2, 2, HT, P], F32R, three)
        d_lo = sb("d_lo", [P, 2, HID], F32R, three)
        hid = sb("hid", [P, 2, SEG], scope=three)
        xres = sb("xres", [P, 2, HID], scope=three)
        xn = sb("xn", [P, 2, HID], scope=three)
        sb("unused", [P, TAB - HID], scope=three)
        h_hi = [sb("h_hi0", [P, 2, SEG], F32R, three)]
        h_lo = [sb("h_lo0", [P, 2, SEG], F32R, three)]
        y2 = sb("y2", [P, TILES, HID], scope=three)
        xn_last = sb("xn_last", [P, CH, HID], scope=three)
        ds = sb("ds", [P, 2, HID], scope=three)[:, 0]
        h_hi.append(sb("h_hi1", [P, 2, SEG], F32R, three))
        h_lo.append(sb("h_lo1", [P, 2, SEG], F32R, three))
        three.close()

        ffn_ps = [proj_ps[0], proj_ps[1], kt_at[0], kt_at[1]]
        ffn_ps_first = [proj_ps[0], proj_ps[1], yp[0], yp[1]]
        w_ffn = w_ints[0:GU_INTS].rearrange("(g p t u r f) -> g p t u r f", p=P, t=2, u=2, r=HT, f=P)
        w_down = w_ints[GU_INTS:].rearrange("(g p f n) -> g p f n", p=P, f=2, n=HID)
        w_blocks = w_ints.rearrange("(c p n) -> c p n", p=P, n=HID)
        x_tiles = x.rearrange("(s t p) h -> s p t h", t=CH, p=P)
        out_tiles = out.rearrange("(s t p) h -> s p t h", t=CH, p=P)
        block = ctx.enter_context(nc.Block())

        def tokens(seg):
            return slice(seg * SEG, (seg + 1) * SEG)

        def chunk(c):
            return slice(c * P, (c + 1) * P)

        norm_a = [NSEG + 2 * s for s in range(NSEG)]
        norm_b = [NSEG + 2 * s + 1 for s in range(NSEG)]
        norm_c = [3 * NSEG + s for s in range(NSEG)]

        def normed_count(number, t):
            return CH * number + t + 1

        @block.sync
        def _(sp):
            def attn_weights(p, kind):
                wait(sp, wlo_done, 4 * p + kind - 1)
                sp.dma_start(raw[:, kind % 2], w_attn[p, kind]).then_inc(raw_in[kind % 2], 16)

            def pair_tables(p):
                wait(sp, table_ready, p)
                sp.dma_start(table_stage[:, :], tables[p]).then_inc(table_in, 16)

            def pair_out_weights(p):
                wait(sp, owlo_done, p)
                sp.dma_start(ow[:, :, :], w_out[p]).then_inc(ow_in, 16)
                sp.dma_start(nw[:, :], norm_w[p]).then_inc(norm_in, 16)

            for t in range(CH):
                sp.dma_start(y[:, t], x_tiles[0, :, t]).then_inc(x_first_in[t], 16)
            attn_weights(0, KK)
            for s in range(1, NSEG):
                sp.dma_start(y[:, s * CH:(s + 1) * CH], x_tiles[s]).then_inc(x_in[s], 16)
                if s == 1:
                    attn_weights(0, QQ)
            attn_weights(0, VV)
            attn_weights(0, GG)
            pair_tables(0)
            pair_out_weights(0)
            with sp.Fori(1, PAIRS) as p:
                attn_weights(p, KK)
                attn_weights(p, QQ)
                pair_tables(p)
                pair_out_weights(p)
                attn_weights(p, VV)
                attn_weights(p, GG)

            def residual(tile):
                wait(sp, mid_added, tile - 1)
                sp.dma_start(xres[:, tile % 2], x_tiles[tile // CH, :, tile % CH])\
                  .then_inc(xres_in[tile % 2], 16)

            def ffn_weights(n):
                wait(sp, flo_done, 2 * n)
                sp.dma_start(fraw[:, :, :, :, :], w_ffn[n]).then_inc(fraw_in, 16)
                wait(sp, fs_ready, n)
                sp.dma_start(fs_stage[:, :], ffn_scales[n]).then_inc(fs_in, 16)
                wait(sp, dlo_done, n)
                sp.dma_start(draw[:, :, :], w_down[n]).then_inc(draw_in, 16)

            sp.wait_ge(wlo_done, 4 * PAIRS)
            sp.dma_start(fraw[:, :, :, :, :], w_ffn[0]).then_inc(fraw_in, 16)
            sp.dma_start(fs_stage[:, :], ffn_scales[0]).then_inc(fs_in, 16)
            sp.wait_ge(owlo_done, PAIRS)
            for tile in range(3 * CH - 2):
                residual(tile)
            sp.wait_ge(proj_done, 8 * STEPS)
            sp.dma_start(draw[:, :, :], w_down[0]).then_inc(draw_in, 16)
            for tile in range(3 * CH - 2, 3 * CH):
                residual(tile)
            sp.wait_ge(ss_done, 2 * STEPS)
            sp.dma_start(ds, down_s.partition_broadcast(P)).then_inc(ds_in, 16)
            sp.wait_ge(yproj_done, 4 * STEPS)
            sp.dma_start(y2[:, 3 * CH:], x_tiles[NSEG - 1]).then_inc(x_last_in, 16)
            with sp.Fori(1, FG) as n:
                ffn_weights(n)
            for s in range(NSEG - 1):
                sp.wait_ge(final_done, CH * (s + 1))
                sp.dma_start(out_tiles[s], y[:, s * CH:(s + 1) * CH]).then_inc(out_sent, 16)
            for t in range(CH):
                sp.wait_ge(last_done, t + 1)
                sp.dma_start(out_tiles[NSEG - 1, :, t], y[:, 3 * CH + t]).then_inc(out_sent, 16)
            sp.wait_ge(out_sent, 16 * (NSEG - 1 + CH))

        @block.gpsimd
        def _(pool):
            def split_lo(p, kind):
                pool.wait_ge(whi_done, 4 * p + kind + 1)
                pool.tensor_tensor(w_lo[:, kind], raw[:, kind % 2], w_hi[:, kind].bitcast(F32),
                                   ALU.subtract).then_inc(wlo_done, 1)

            def split_out_lo(p):
                pool.wait_ge(owhi_done, p + 1)
                pool.tensor_tensor(ow_lo[:, :, :], ow[:, :, :], ow_hi[:, :, :].bitcast(F32),
                                   ALU.subtract).then_inc(owlo_done, 1)

            def query_decay(a):
                for h in range(2):
                    pool.wait_ge(silu_done, 6 * a + 3 + h)
                    wait(pool, attn_done, 2 * a + h - 1)
                    decay = table[:, TAB_Q + h * P:TAB_Q + (h + 1) * P]
                    pool.tensor_tensor(qd[:, h].rearrange("p (c n) -> p c n", c=CH),
                                       q[:, h].rearrange("p (c n) -> p c n", c=CH),
                                       decay.unsqueeze(1).to_broadcast([P, CH, P]),
                                       ALU.mult).then_inc(qd_done, 1)

            def add_squares(a, seg):
                for h in range(2):
                    pool.wait_ge(sq_done, 2 * a + h + 1)
                    wait(pool, ss_done, 2 * a + h)
                    pool.tensor_tensor(sumsq[:, tokens(seg)], sumsq[:, tokens(seg)], sq[:, h],
                                       ALU.add).then_inc(ss_done, 1)

            def gated_lo(a):
                for h in range(2):
                    pool.wait_ge(ghi_done, 2 * a + h + 1)
                    pool.tensor_tensor(g_lo[:, h], g[:, h], g_hi[:, h].bitcast(F32),
                                       ALU.subtract).then_inc(glo_done, 1)

            def attention(a, seg):
                query_decay(a)
                add_squares(a, seg)
                gated_lo(a)

            pool.memset(ident[:, :], 0.0).then_inc(const_done, 1)
            pool.wait_ge(const_done, 1)
            pool.affine_select(out=ident[:, :], in_=ident[:, :], compare_op=ALU.not_equal, fill=1.0,
                               base=0, pattern=[[-1, P]], channel_multiplier=1).then_inc(const_done, 1)
            pool.memset(ones[:, :], 1.0).then_inc(const_done, 1)
            pool.memset(sumsq[:, :], 0.0).then_inc(ss_cleared, 1)
            for kind in range(4):
                split_lo(0, kind)
            for s in range(NSEG):
                pool.wait_ge(xt_done, CH * (s + 1))
                pool.memset(y[:, s * CH:(s + 1) * CH].rearrange("p t h -> p (t h)"), 0.0)\
                    .then_inc(y_cleared, 1)
            pool.wait_ge(ss_cleared, 1)
            pool.wait_ge(table_ready, 1)
            attention(0, 0)
            split_out_lo(0)
            with pool.Fori(0, PAIRS - 1) as i:
                for j in range(NSEG):
                    a = 4 * i + 1 + j
                    if j == 3:
                        pool.wait_ge(table_ready, i + 2)
                    attention(a, (1 + j) % NSEG)
                    if j == 1:
                        for kind in range(4):
                            split_lo(i + 1, kind)
                    if j == 3:
                        split_out_lo(i + 1)

            def add_residual(s):
                if s == NSEG - 1:
                    pool.wait_ge(x_last_in, 16)
                for t in range(CH):
                    tile = s * CH + t
                    pool.wait_ge(normed, normed_count(norm_a[s], t))
                    if s < NSEG - 1:
                        pool.wait_ge(xres_in[tile % 2], 16 * (tile // 2 + 1))
                    again = xres[:, tile % 2] if s < NSEG - 1 else y2[:, tile]
                    pool.tensor_tensor(y[:, tile], y[:, tile], again, ALU.add).then_inc(mid_added, 1)

            def ffn_split_lo(n, t):
                pool.wait_ge(fcv_done, 2 * n + t + 1)
                pool.tensor_tensor(f_lo[:, t], fraw[:, t].bitcast(F32), f_hi[:, t].bitcast(F32),
                                   ALU.subtract).then_inc(flo_done, 1)

            def down_split_lo(n):
                pool.wait_ge(dcv_done, n + 1)
                pool.tensor_tensor(d_lo[:, :, :], draw[:, :, :].bitcast(F32),
                                   d_hi[:, :, :].bitcast(F32), ALU.subtract).then_inc(dlo_done, 1)

            def hidden_lo(m, par, t):
                pool.wait_ge(hhi_done, 2 * m + t + 1)
                pool.tensor_tensor(h_lo[par][:, t], hid[:, t], h_hi[par][:, t].bitcast(F32),
                                   ALU.subtract).then_inc(hlo_done, 1)

            def hidden(m, par, split=None):
                for t in range(2):
                    hidden_lo(m, par, t)
                    if split is not None:
                        ffn_split_lo(split, t)

            def last_residual(s):
                for t in range(CH):
                    tile = s * CH + t
                    pool.wait_ge(normed, normed_count(norm_c[s], t))
                    pool.tensor_tensor(y[:, tile], y[:, tile], y2[:, tile],
                                       ALU.add).then_inc(final_done, 1)

            pool.wait_ge(part_done, 1)
            pool.partition_all_reduce(all_max[:, :], part_max[:, :], P,
                                      bass.bass_isa.ReduceOp.max).then_inc(all_max_done, 1)
            query_decay(STEPS - 3)
            add_residual(0)
            add_squares(STEPS - 3, 1)
            gated_lo(STEPS - 3)
            query_decay(STEPS - 2)
            add_residual(1)
            ffn_split_lo(0, 0)
            add_squares(STEPS - 2, 2)
            gated_lo(STEPS - 2)
            ffn_split_lo(0, 1)
            query_decay(STEPS - 1)
            pool.wait_ge(qd_done, 2 * STEPS)
            hidden_lo(0, 0, 0)
            add_residual(2)
            add_squares(STEPS - 1, 3)
            gated_lo(STEPS - 1)
            hidden_lo(0, 0, 1)
            down_split_lo(0)
            hidden(1, 1)
            add_residual(3)
            hidden(2, 0)
            pool.wait_ge(mid_added, TILES)
            pool.memset(y2[:, 3 * CH:].rearrange("p t h -> p (t h)"), 0.0).then_inc(y2_cleared, 1)
            hidden(3, 1, split=1)
            with pool.Fori(1, FG - 1) as i:
                for j in range(NSEG):
                    if j == 1:
                        down_split_lo(i)
                    hidden(4 * i + j, j % 2, split=i + 1 if j == 3 else None)
            for j in range(NSEG):
                if j == 1:
                    down_split_lo(FG - 1)
                if j == 3:
                    last_residual(0)
                hidden(FSTEPS - NSEG + j, j % 2)
            last_residual(1)
            last_residual(2)

        @block.scalar
        def _(act):
            def square_root(number):
                act.wait_ge(var_ready, number + 1)
                act.activation(stdev[:, number % 4], var_eps[:, number % 4],
                               ACT.Sqrt).then_inc(sd_ready, 1)

            def normalise(src, dst, number, tiles=range(CH)):
                act.wait_ge(scale_ready, number + 1)
                for t in tiles:
                    act.activation(dst(t), src(t), ACT.Identity,
                                   bias=shift[:, number % 4, t:t + 1],
                                   scale=rstd[:, number % 4, t:t + 1]).then_inc(normed, 1)

            def x_hi_part(t, psum, count):
                act.wait_ge(xt_done, count + 1)
                act.activation(x_hi[:, :, chunk(t)], psum[:, :].rearrange("p (h n) -> p h n", h=HT),
                               ACT.Copy).then_inc(xhi_done, 1)

            def split_hi(p, kind, n):
                act.wait_ge(raw_in[kind % 2], 32 * p + 16 * (kind // 2) + 16)
                if n is not None:
                    act.wait_ge(proj_done, 8 * n + (2, 4, 6, 8)[kind])
                act.activation(w_hi[:, kind], raw[:, kind % 2], ACT.Copy).then_inc(whi_done, 1)

            def split_out_hi(p, a):
                act.wait_ge(ow_scaled, 2 * p + 2)
                wait(act, yproj_done, 4 * a)
                act.activation(ow_hi[:, :, :], ow[:, :, :], ACT.Copy).then_inc(owhi_done, 1)

            def sigmoid(n, u):
                act.wait_ge(proj_done, 8 * n + u + 1)
                a = n - 1
                h = u % 2
                if u < 2:
                    wait(act, score_done, 2 * a + h + 1)
                    dst, src = k[:, h], proj_ps[h][:, :]
                elif u < 4:
                    wait(act, score_done, 2 * a + h + 1)
                    wait(act, qd_done, 2 * a + h + 1)
                    dst, src = q[:, h], proj_ps[h][:, :]
                elif u < 6:
                    wait(act, attn_done, 2 * a + 2)
                    dst = v[:, 2 * h:2 * h + 2].rearrange("p c h d -> p (c h d)")
                    src = proj_ps[h][:, :]
                else:
                    wait(act, glo_done, 2 * a + h + 1)
                    dst, src = g[:, h], proj_ps[h][:, :]
                act.activation(dst, src, ACT.Sigmoid).then_inc(sig_done, 1)

            def k_decay(a, h):
                act.wait_ge(kt_done, 2 * a + h + 1)
                wait(act, contrib_done, 2 * a + h - 1)
                act.activation(kd[:, h].rearrange("p c d -> p (c d)"), kt_at[h][:, :], ACT.Copy,
                               scale=table[:, TAB_K + h:TAB_K + h + 1]).then_inc(kd_done, 1)

            def square(a, h):
                act.wait_ge(attn_done, 2 * a + h + 1)
                wait(act, ss_done, 2 * a + h - 1)
                act.activation(sq[:, h], kt_at[h][:, :], ACT.Square).then_inc(sq_done, 1)

            def gated_hi(a, h):
                act.wait_ge(gated_done, 2 * a + h + 1)
                wait(act, yproj_done, 4 * a)
                act.activation(g_hi[:, h], g[:, h], ACT.Copy).then_inc(ghi_done, 1)

            def step(a, n, table_count=None, split=None, out_split=None):
                if table_count is not None:
                    act.wait_ge(table_ready, table_count)
                for h in range(2):
                    k_decay(a, h)
                    sigmoid(n, h)
                sigmoid(n, 2)
                sigmoid(n, 3)
                square(a, 0)
                square(a, 1)
                if out_split is not None:
                    split_out_hi(out_split, a)
                gated_hi(a, 0)
                gated_hi(a, 1)
                for u in range(4, 8):
                    sigmoid(n, u)
                    if split is not None:
                        split_hi(split, (KK, QQ, VV, GG)[u - 4], n)

            def y_tile(s):
                return lambda t: y[:, s * CH + t]

            square_root(0)
            normalise(y_tile(0), y_tile(0), 0)
            split_hi(0, KK, None)
            for t in range(CH):
                x_hi_part(t, ln1_ring[t % 6], t)
            square_root(1)
            normalise(y_tile(1), y_tile(1), 1)
            split_hi(0, QQ, None)
            for u in range(8):
                sigmoid(0, u)
                for t in range(CH + 2 * u, min(CH + 2 * u + 2, TILES)):
                    x_hi_part(t, ln1_ring[t % 6], t)
                if u in (0, 2):
                    s = 2 + u // 2
                    square_root(s)
                    normalise(y_tile(s), y_tile(s), s)
                if u in (1, 3):
                    split_hi(0, VV if u == 1 else GG, None)

            def four_steps(i, checks):
                for j in range(NSEG):
                    a = 4 * i + 1 + j
                    if checks and j < CHECKS_PER_PAIR:
                        c = CHECKS_PER_PAIR * i + j
                        act.wait_ge(block_done, c)
                        act.dma_start(check[:, :], w_blocks[c]).then_inc(check_in, 16)
                    step(a, a + 1, table_count=i + 2 if j == 3 else None,
                         split=i + 1 if j == 1 else None, out_split=i + 1 if j == 3 else None)

            step(0, 1, table_count=1, out_split=0)
            with act.Fori(0, CHECK_PAIRS) as i:
                four_steps(i, True)
            with act.Fori(CHECK_PAIRS, PAIRS - 1) as i:
                four_steps(i, False)

            def normalise_a(s):
                normalise(y_tile(s), y_tile(s), norm_a[s])

            def normalise_b(s, tiles):
                if s == NSEG - 1:
                    act.wait_ge(yproj_done, 4 * STEPS)
                    normalise(y_tile(s), lambda t: xn_last[:, t], norm_b[s], tiles)
                    return
                act.wait_ge(xt_done, TILES + CH * s + tiles[0])
                normalise(y_tile(s), lambda t: xn[:, t % 2], norm_b[s], tiles)

            def mid_hi(s, tiles):
                for t in tiles:
                    x_hi_part(s * CH + t, sc_st[t % 2], TILES + s * CH + t)

            def ffn_split_hi(n, t, m):
                act.wait_ge(fraw_in, 16 * (n + 1))
                if m is not None:
                    act.wait_ge(fproj_done, 4 * m + 2 * t + 2)
                else:
                    act.wait_ge(proj_done, 8 * (STEPS - 1) + 2 * t + 2)
                act.activation(f_hi[:, t], fraw[:, t], ACT.Copy).then_inc(fhi_done, 1)
                act.wait_ge(fhi_done, 2 * n + t + 1)
                act.activation(fraw[:, t].bitcast(F32), fraw[:, t], ACT.Copy).then_inc(fcv_done, 1)

            def down_split_hi(n, d):
                act.wait_ge(draw_in, 16 * (n + 1))
                wait(act, down_done, 4 * d)
                act.activation(d_hi[:, :, :], draw[:, :, :], ACT.Copy).then_inc(dhi_done, 1)
                act.wait_ge(dhi_done, n + 1)
                act.activation(draw[:, :, :].bitcast(F32), draw[:, :, :], ACT.Copy)\
                    .then_inc(dcv_done, 1)

            def ffn_sigmoid(m, t, psum=ffn_ps):
                act.wait_ge(fproj_done, 4 * m + 2 * t + 1)
                wait(act, hlo_done, 2 * m + t - 1)
                act.activation(hid[:, t], psum[2 * t][:, :], ACT.Sigmoid,
                               scale=fs[:, t:t + 1]).then_inc(fsig_done, 1)

            def hidden_hi(m, par, t):
                act.wait_ge(hid_done, 2 * m + t + 1)
                wait(act, down_done, 4 * (m - 1))
                act.activation(h_hi[par][:, t], hid[:, t], ACT.Copy).then_inc(hhi_done, 1)

            def late_step(a, s):
                n = a + 1
                k_decay(a, 0)
                sigmoid(n, 0)
                k_decay(a, 1)
                sigmoid(n, 1)
                square_root(norm_a[s])
                normalise_a(s)
                sigmoid(n, 2)
                if n == STEPS - 1:
                    ffn_split_hi(0, 0, None)
                sigmoid(n, 3)
                square(a, 0)
                square(a, 1)
                square_root(norm_b[s])
                gated_hi(a, 0)
                gated_hi(a, 1)
                sigmoid(n, 4)
                normalise_b(s, (0, 1))
                sigmoid(n, 5)
                mid_hi(s, (0, 1))
                normalise_b(s, (2, 3))
                sigmoid(n, 6)
                mid_hi(s, (2, 3))
                if n == STEPS - 1:
                    ffn_split_hi(0, 1, None)
                sigmoid(n, 7)

            late_step(STEPS - 3, 0)
            late_step(STEPS - 2, 1)
            last = STEPS - 1
            k_decay(last, 0)
            square_root(norm_a[2])
            act.wait_ge(fs_ready, 1)
            ffn_sigmoid(0, 0, ffn_ps_first)
            k_decay(last, 1)
            act.wait_ge(score_done, 2 * STEPS)
            hidden_hi(0, 0, 0)
            normalise_a(2)
            down_split_hi(0, 0)
            ffn_sigmoid(0, 1, ffn_ps_first)
            square(last, 0)
            square(last, 1)
            hidden_hi(0, 0, 1)
            square_root(norm_b[2])
            gated_hi(last, 0)
            gated_hi(last, 1)
            ffn_sigmoid(1, 0)
            normalise_b(2, (0, 1))
            act.wait_ge(ssum_done, NSEG)
            hidden_hi(1, 1, 0)
            ffn_sigmoid(1, 1)
            hidden_hi(1, 1, 1)
            mid_hi(2, (0, 1))
            normalise_b(2, (2, 3))
            square_root(norm_a[3])
            normalise_a(3)
            mid_hi(2, (2, 3))
            ffn_sigmoid(2, 0)
            hidden_hi(2, 0, 0)
            ffn_sigmoid(2, 1)
            hidden_hi(2, 0, 1)
            square_root(norm_b[3])
            normalise_b(3, range(CH))
            mid_hi(3, range(CH))

            def ffn_step(m, par, scales=None, split=None, down=None):
                if scales is not None:
                    act.wait_ge(fs_ready, scales)
                if down is not None:
                    down_split_hi(down, m - 1)
                for t in range(2):
                    ffn_sigmoid(m, t)
                    hidden_hi(m, par, t)
                    if split is not None:
                        ffn_split_hi(split, t, m)

            ffn_step(3, 1, split=1)
            with act.Fori(1, FG - 1) as i:
                for j in range(NSEG):
                    ffn_step(4 * i + j, j % 2, scales=i + 1 if j == 0 else None,
                             split=i + 1 if j == 3 else None, down=i if j == 1 else None)

            def final_norm(s):
                square_root(norm_c[s])
                normalise(lambda t: y2[:, s * CH + t], lambda t: y2[:, s * CH + t], norm_c[s])

            for j in range(NSEG):
                if j == 3:
                    final_norm(0)
                ffn_step(FSTEPS - NSEG + j, j % 2, scales=FG if j == 0 else None,
                         down=FG - 1 if j == 1 else None)
            for s in range(1, NSEG):
                final_norm(s)

        @block.vector
        def _(dve):
            own = [0]

            def norm_statistics(src, number, extra=None, arrived=None):
                z = number % 4
                for t in range(CH):
                    if arrived is not None:
                        dve.wait_ge(arrived[t], 16)
                    dve.bn_stats(stats[:, z, t], src(t)).then_inc(ln_own, 1)
                own[0] += CH
                dve.wait_ge(ln_own, own[0])
                for t in range(CH):
                    dve.bn_aggr(meanvar[:, z, t], stats[:, z, t]).then_inc(ln_own, 1)
                own[0] += CH
                dve.wait_ge(ln_own, own[0])
                if extra is None:
                    dve.tensor_scalar(var_eps[:, z], meanvar[:, z, :, 1], LN_EPS, None,
                                      ALU.add).then_inc(var_ready, 1)
                else:
                    dve.tensor_tensor(var_eps[:, z], meanvar[:, z, :, 1], extra,
                                      ALU.add).then_inc(var_ready, 1)

            def norm_scales(number):
                z = number % 4
                dve.wait_ge(sd_ready, number + 1)
                dve.reciprocal(rstd[:, z], stdev[:, z]).then_inc(ln_own, 1)
                own[0] += 1
                dve.wait_ge(ln_own, own[0])
                dve.scalar_tensor_tensor(shift[:, z], meanvar[:, z, :, 0], -1.0, rstd[:, z],
                                         ALU.mult, ALU.mult).then_inc(scale_ready, 1)

            def x_lo_part(t, psum, count):
                dve.wait_ge(xhi_done, count + 1)
                dve.tensor_tensor(x_lo[:, :, chunk(t)], psum[:, :].rearrange("p (h n) -> p h n", h=HT),
                                  x_hi[:, :, chunk(t)].bitcast(F32), ALU.subtract).then_inc(xlo_done, 1)

            def next_table(a, p):
                wait(dve, kd_done, 2 * a)
                wait(dve, qd_done, 2 * a)
                dve.wait_ge(table_in, 16 * (p + 1))
                dve.tensor_copy(table[:, :], table_stage[:, :]).then_inc(table_ready, 1)
                dve.wait_ge(table_ready, p + 1)

            def scale_out_weights(p):
                dve.wait_ge(ow_in, 16 * (p + 1))
                dve.wait_ge(norm_in, 16 * (p + 1))
                for h in range(2):
                    dve.tensor_scalar(ow[:, h], ow[:, h], nw[:, h:h + 1], None,
                                      ALU.mult).then_inc(ow_scaled, 1)

            def silu(n, u):
                dve.wait_ge(sig_done, 8 * n + u + 1)
                h = u % 2
                dst = (k[:, h], q[:, h], v[:, 2 * h:2 * h + 2].rearrange("p c h d -> p (c h d)"))[u // 2]
                dve.tensor_tensor(dst, proj_ps[h][:, :], dst, ALU.mult).then_inc(silu_done, 1)

            def decay_scores(a, h):
                dve.wait_ge(score_done, 2 * a + h + 1)
                wait(dve, attn_done, 2 * a + h - 1)
                mask = table[:, TAB_D + h * P:TAB_D + (h + 1) * P]
                dve.tensor_tensor(pd[:, h], sc_st[h][:, :].rearrange("p (c n) -> p c n", c=CH),
                                  mask.unsqueeze(1).to_broadcast([P, CH, P]),
                                  ALU.mult).then_inc(pdec_done, 1)

            def update_state(a, odd, h):
                dve.wait_ge(contrib_done, 2 * a + h + 1)
                done = states_before(a, odd) + h * (CH - odd)
                for c in range(CH - odd):
                    new = sc_st[h][:, chunk(c)]
                    if c == 0 and not odd:
                        dve.tensor_copy(state[:, h, 0], new).then_inc(state_done, 1)
                        continue
                    wait(dve, state_done, done + c)
                    dve.scalar_tensor_tensor(state[:, h, c], state[:, h, (c - 1) % CH],
                                             table[:, TAB_B + h:TAB_B + h + 1], new,
                                             ALU.mult, ALU.add).then_inc(state_done, 1)

            def gate(a, h):
                dve.wait_ge(sq_done, 2 * a + h + 1)
                dve.wait_ge(sig_done, 8 * a + 7 + h)
                dve.tensor_tensor(g[:, h], kt_at[h][:, :], g[:, h], ALU.mult).then_inc(gated_done, 1)

            def add_out(a, seg, t):
                dve.wait_ge(yproj_done, 4 * a + t + 1)
                tile = y[:, seg * CH + t]
                dve.tensor_tensor(tile, yp[t % 2][:, :], tile, ALU.add).then_inc(yacc_done, 1)

            def step(a, seg, n, pair=None):
                odd = seg % 2
                if pair is not None:
                    next_table(a, pair)
                for h in range(2):
                    decay_scores(a, h)
                    silu(n, h)
                update_state(a, odd, 0)
                update_state(a, odd, 1)
                silu(n, 2)
                silu(n, 3)
                if pair is not None:
                    scale_out_weights(pair)
                gate(a, 0)
                gate(a, 1)
                silu(n, 4)
                silu(n, 5)
                for t in range(CH):
                    add_out(a, seg, t)

            def y_tile(s):
                return lambda t: y[:, s * CH + t]

            norm_statistics(y_tile(0), 0, arrived=x_first_in)
            norm_scales(0)
            dve.wait_ge(x_in[1], 16)
            norm_statistics(y_tile(1), 1)
            for t in range(CH):
                x_lo_part(t, ln1_ring[t % 6], t)
            norm_scales(1)
            for s in range(2, NSEG):
                dve.wait_ge(x_in[s], 16)
                norm_statistics(y_tile(s), s)
            for u in range(8):
                if u < 6:
                    silu(0, u)
                for t in range(CH + 2 * u, min(CH + 2 * u + 2, TILES)):
                    x_lo_part(t, ln1_ring[t % 6], t)
                if u in (0, 2):
                    norm_scales(2 + u // 2)

            def look_at_block(c, j):
                dve.wait_ge(check_in, 16 * (c + 1))
                dve.wait_ge(max_done, c)
                dve.tensor_reduce(block_max[:, j:j + 1], check[:, :], AX.X, ALU.max,
                                  apply_absolute_value=True).then_inc(block_done, 1)
                dve.wait_ge(block_done, c + 1)
                dve.tensor_tensor(ints_max[:, j:j + 1], ints_max[:, j:j + 1], block_max[:, j:j + 1],
                                  ALU.max).then_inc(max_done, 1)

            def four_steps(i, checks):
                for j in range(NSEG):
                    a = 4 * i + 1 + j
                    step(a, (1 + j) % NSEG, a + 1, pair=i + 1 if j == 3 else None)
                    if checks and j < CHECKS_PER_PAIR:
                        look_at_block(CHECKS_PER_PAIR * i + j, j)

            dve.memset(ints_max[:, :], 0.0).then_inc(max_cleared, 1)
            dve.wait_ge(y_cleared, 1)
            step(0, 0, 1, pair=0)
            dve.wait_ge(y_cleared, NSEG)
            dve.wait_ge(max_cleared, 1)
            with dve.Fori(0, CHECK_PAIRS) as i:
                four_steps(i, True)
            dve.wait_ge(max_done, WIDTH_CHECKS)
            dve.tensor_reduce(part_max[:, :], ints_max[:, :], AX.X, ALU.max).then_inc(part_done, 1)
            with dve.Fori(CHECK_PAIRS, PAIRS - 1) as i:
                four_steps(i, False)
            def rms(s, psum):
                dve.wait_ge(ssum_done, s + 1)
                dve.tensor_scalar(rms_term[:, s * CH:(s + 1) * CH], psum[:, 0:CH],
                                  LN_EPS / (HEADS * HD), LN_EPS * RMS_EPS,
                                  ALU.mult, ALU.add).then_inc(rms_ready, 1)

            def statistics_a(s):
                dve.wait_ge(rms_ready, s + 1)
                dve.wait_ge(yacc_done, 4 * (STEPS - NSEG + s + 1))
                norm_statistics(y_tile(s), norm_a[s], extra=rms_term[:, s * CH:(s + 1) * CH])

            def statistics_b(s):
                dve.wait_ge(mid_added, CH * (s + 1))
                norm_statistics(y_tile(s), norm_b[s])

            def mid_lo(s, tiles):
                for t in tiles:
                    x_lo_part(s * CH + t, sc_st[t % 2], TILES + s * CH + t)

            def late_step(a, seg, s):
                n = a + 1
                decay_scores(a, 0)
                silu(n, 0)
                rms(s, yp[0])
                statistics_a(s)
                decay_scores(a, 1)
                silu(n, 1)
                norm_scales(norm_a[s])
                update_state(a, seg % 2, 0)
                update_state(a, seg % 2, 1)
                silu(n, 2)
                silu(n, 3)
                statistics_b(s)
                gate(a, 0)
                gate(a, 1)
                norm_scales(norm_b[s])
                silu(n, 4)
                silu(n, 5)
                mid_lo(s, range(CH))
                for t in range(CH):
                    add_out(a, seg, t)

            def new_scales(n):
                wait(dve, hid_done, 2 * NSEG * n)
                dve.wait_ge(fs_in, 16 * (n + 1))
                dve.tensor_copy(fs[:, :], fs_stage[:, :]).then_inc(fs_ready, 1)
                dve.wait_ge(fs_ready, n + 1)

            def hidden(m, t, psum=ffn_ps):
                dve.wait_ge(fsig_done, 2 * m + t + 1)
                dve.scalar_tensor_tensor(hid[:, t], psum[2 * t][:, :], fs[:, t:t + 1], hid[:, t],
                                         ALU.mult, ALU.mult).then_inc(fgate_done, 1)
                dve.wait_ge(fproj_done, 4 * m + 2 * t + 2)
                dve.wait_ge(fgate_done, 2 * m + t + 1)
                dve.scalar_tensor_tensor(hid[:, t], psum[2 * t + 1][:, :], fs[:, 2 + t:3 + t],
                                         hid[:, t], ALU.mult, ALU.mult).then_inc(hid_done, 1)

            def add_down(d, seg, t, first=False):
                dve.wait_ge(down_done, 4 * d + t + 1)
                tile = y2[:, seg * CH + t]
                if first:
                    dve.tensor_copy(tile, yp[t % 2][:, :]).then_inc(y2acc_done, 1)
                else:
                    dve.tensor_tensor(tile, yp[t % 2][:, :], tile, ALU.add).then_inc(y2acc_done, 1)

            dve.wait_ge(all_max_done, 1)
            dve.tensor_scalar(wide[:, :], all_max[:, :], F32R_EXACT, None,
                              ALU.is_gt).then_inc(wide_ready, 1)
            late_step(STEPS - 3, 1, 0)
            late_step(STEPS - 2, 2, 1)
            last = STEPS - 1
            decay_scores(last, 0)
            new_scales(0)
            rms(2, yp[0])
            statistics_a(2)
            hidden(0, 0, ffn_ps_first)
            decay_scores(last, 1)
            norm_scales(norm_a[2])
            update_state(last, 1, 0)
            update_state(last, 1, 1)
            hidden(0, 1, ffn_ps_first)
            statistics_b(2)
            gate(last, 0)
            gate(last, 1)
            norm_scales(norm_b[2])
            hidden(1, 0)
            rms(3, sc_st[0])
            hidden(1, 1)
            for t in range(CH):
                add_out(last, NSEG - 1, t)
            statistics_a(3)
            mid_lo(2, (0,))
            norm_scales(norm_a[3])
            mid_lo(2, (1,))
            for t in range(CH):
                add_down(0, 0, t, first=True)
            mid_lo(2, (2, 3))
            hidden(2, 0)
            statistics_b(3)
            hidden(2, 1)
            norm_scales(norm_b[3])
            for t in range(CH):
                add_down(1, 1, t, first=True)
            mid_lo(3, range(CH))
            hidden(3, 0)
            hidden(3, 1)
            for t in range(CH):
                add_down(2, 2, t, first=True)
            dve.wait_ge(y2_cleared, 1)

            def ffn_step(m, d, seg, scales=None):
                if scales is not None:
                    new_scales(scales)
                for t in range(2):
                    hidden(m, t)
                    add_down(d, seg, 2 * t)
                    add_down(d, seg, 2 * t + 1)

            def statistics_c(s):
                dve.wait_ge(y2acc_done, NSEG * CH * (FG - 1) + CH * (s + 1))
                for t in range(CH):
                    dve.tensor_tensor(y2[:, s * CH + t], y2[:, s * CH + t], ds,
                                      ALU.mult).then_inc(ln_own, 1)
                own[0] += CH
                dve.wait_ge(ln_own, own[0])
                norm_statistics(lambda t: y2[:, s * CH + t], norm_c[s])

            with dve.Fori(1, FG - 1) as i:
                for j in range(NSEG):
                    m = 4 * i + j
                    ffn_step(m, m - 1, (j - 1) % NSEG, scales=i if j == 0 else None)
            dve.wait_ge(ds_in, 16)
            first = FSTEPS - NSEG
            ffn_step(first, first - 1, 3, scales=FG - 1)
            ffn_step(first + 1, first, 0)
            statistics_c(0)
            ffn_step(first + 2, first + 1, 1)
            norm_scales(norm_c[0])
            statistics_c(1)
            for t in range(2):
                hidden(first + 3, t)
            norm_scales(norm_c[1])
            for t in range(CH):
                add_down(first + 2, 2, t)
            statistics_c(2)
            for t in range(CH):
                add_down(first + 3, 3, t)
            norm_scales(norm_c[2])
            statistics_c(3)
            norm_scales(norm_c[3])
            for t in range(CH):
                dve.wait_ge(normed, normed_count(norm_c[3], t))
                tile = 3 * CH + t
                dve.tensor_tensor(y[:, tile], y[:, tile], y2[:, tile], ALU.add).then_inc(last_done, 1)

        @block.tensor
        def _(pe):
            def split_product(psum, stationary, moving, done=None, drop=None):
                terms = []
                for s, m in zip(stationary, moving):
                    terms.append((s[0], m[0]))
                    if drop != "moving":
                        terms.append((s[0], m[1]))
                    if drop != "stationary":
                        terms.append((s[1], m[0]))
                for n, (s, m) in enumerate(terms):
                    last = pe.matmul(psum, s, m, start=n == 0, stop=n == len(terms) - 1)
                if done is not None:
                    last.then_inc(done, 1)

            def transpose_x(t, src, psum, count):
                pe.wait_ge(normed, count)
                for h in range(HT):
                    last = pe.transpose(psum[:, chunk(h)], src[:, chunk(h)], ident[:, :])
                last.then_inc(xt_done, 1)

            def unit(n, seg, u, new_pair=None):
                if new_pair is not None and u in (0, 2, 4, 6):
                    pe.wait_ge(wlo_done, 4 * new_pair + u // 2 + 1)
                if u < 2:
                    wait(pe, sig_done, 8 * n - 1 + u)
                else:
                    pe.wait_ge(silu_done, 6 * n + u - 1)
                h = u % 2
                if u in (4, 5):
                    for c in range(2):
                        tok = slice(seg * SEG + (2 * h + c) * P, seg * SEG + (2 * h + c + 1) * P)
                        split_product(
                            proj_ps[h][:, c * 2 * HD:(c + 1) * 2 * HD],
                            [(x_hi[:, r, tok], x_lo[:, r, tok]) for r in range(HT)],
                            [(w_hi[:, VV, r].rearrange("p h d -> p (h d)"),
                              w_lo[:, VV, r].rearrange("p h d -> p (h d)")) for r in range(HT)],
                            proj_done if c == 1 else None)
                    return
                kind = (KK, QQ, VV, GG)[u // 2]
                split_product(proj_ps[h][:, :],
                              [(w_hi[:, kind, r, h], w_lo[:, kind, r, h]) for r in range(HT)],
                              [(x_hi[:, r, tokens(seg)], x_lo[:, r, tokens(seg)]) for r in range(HT)],
                              proj_done)

            def transposes_and_scores(a, h):
                pe.wait_ge(silu_done, 6 * a + 3 + h)
                wait(pe, gated_done, 2 * a + h - 1)
                for c in range(CH):
                    last = pe.transpose(kt_at[h][:, chunk(c)], k[:, h, chunk(c)], ident[:, :])
                last.then_inc(kt_done, 1)
                for c in range(CH):
                    last = pe.matmul(sc_st[h][:, chunk(c)], k[:, h, chunk(c)], q[:, h, chunk(c)],
                                     start=True, stop=True)
                last.then_inc(score_done, 1)

            def contributions(a, odd, h):
                pe.wait_ge(silu_done, 6 * a + 6)
                pe.wait_ge(kd_done, 2 * a + h + 1)
                pe.wait_ge(pdec_done, 2 * a + h + 1)
                for c in range(CH - odd):
                    last = pe.matmul(sc_st[h][:, chunk(c)], kd[:, h, c], v[:, c, h],
                                     start=True, stop=True)
                last.then_inc(contrib_done, 1)

            def attend(a, odd, h):
                pe.wait_ge(qd_done, 2 * a + h + 1)
                pe.wait_ge(state_done, states_before(a, odd) + (h + 1) * (CH - odd))
                for c in range(CH):
                    inter = c > 0 or odd
                    last = pe.matmul(kt_at[h][:, chunk(c)], v[:, c, h], pd[:, h, c],
                                     start=True, stop=not inter)
                    if inter:
                        last = pe.matmul(kt_at[h][:, chunk(c)], state[:, h, (c - 1) % CH],
                                         qd[:, h, chunk(c)], start=False, stop=True)
                last.then_inc(attn_done, 1)

            def project_out(a, t, new_pair=None):
                if t == 0:
                    pe.wait_ge(glo_done, 2 * a + 2)
                    if new_pair is not None:
                        pe.wait_ge(owlo_done, new_pair + 1)
                wait(pe, yacc_done, 4 * a + t - 1)
                split_product(yp[t % 2][:, :],
                              [(g_hi[:, h, chunk(t)], g_lo[:, h, chunk(t)]) for h in range(2)],
                              [(ow_hi[:, h], ow_lo[:, h]) for h in range(2)],
                              yproj_done)

            def sums_of_squares(s, psum):
                pe.wait_ge(ss_done, 2 * (STEPS - NSEG + s + 1))
                if s < NSEG - 1:
                    pe.wait_ge(yacc_done, 4 * (STEPS - NSEG + s + 1) - 1)
                for t in range(CH):
                    last = pe.matmul(psum[:, t:t + 1], sumsq[:, chunk(s * CH + t)], ones[:, :],
                                     start=True, stop=True)
                last.then_inc(ssum_done, 1)

            def mid_transposes(s, tiles):
                for t in tiles:
                    tile = s * CH + t
                    wait(pe, xlo_done, TILES + tile - 1)
                    src = xn[:, t % 2] if s < NSEG - 1 else xn_last[:, t]
                    transpose_x(tile, src, sc_st[t % 2], normed_count(norm_b[s], t))

            def step(a, seg, n, pair_n=None, pair_a=None):
                odd = seg % 2
                seg_n = (seg + 1) % NSEG
                transposes_and_scores(a, 0)
                unit(n, seg_n, 0, pair_n)
                transposes_and_scores(a, 1)
                unit(n, seg_n, 1, pair_n)
                contributions(a, odd, 0)
                contributions(a, odd, 1)
                unit(n, seg_n, 2, pair_n)
                unit(n, seg_n, 3, pair_n)
                attend(a, odd, 0)
                attend(a, odd, 1)
                unit(n, seg_n, 4, pair_n)
                unit(n, seg_n, 5, pair_n)
                unit(n, seg_n, 6, pair_n)
                project_out(a, 0, pair_a)
                project_out(a, 1)
                unit(n, seg_n, 7, pair_n)
                project_out(a, 2)
                project_out(a, 3)

            def late_step(a, seg, s):
                n, odd = a + 1, seg % 2
                wait(pe, xlo_done, TILES + CH * s)
                transposes_and_scores(a, 0)
                unit(n, seg + 1, 0)
                sums_of_squares(s, yp[0])
                transposes_and_scores(a, 1)
                unit(n, seg + 1, 1)
                contributions(a, odd, 0)
                contributions(a, odd, 1)
                unit(n, seg + 1, 2)
                unit(n, seg + 1, 3)
                attend(a, odd, 0)
                attend(a, odd, 1)
                unit(n, seg + 1, 4)
                unit(n, seg + 1, 5)
                mid_transposes(s, (0, 1))
                unit(n, seg + 1, 6)
                mid_transposes(s, (2, 3))
                pe.wait_ge(rms_ready, s + 1)
                project_out(a, 0)
                project_out(a, 1)
                unit(n, seg + 1, 7)
                project_out(a, 2)
                project_out(a, 3)

            pe.wait_ge(const_done, 3)
            for t in range(CH):
                transpose_x(t, y[:, t], ln1_ring[t], t + 1)
            pe.wait_ge(xlo_done, CH)
            for u in range(8):
                unit(0, 0, u, 0)
                for t in range(CH + 2 * u, min(CH + 2 * u + 2, TILES)):
                    wait(pe, xlo_done, t - 5)
                    transpose_x(t, y[:, t], ln1_ring[t % 6], t + 1)
            pe.wait_ge(xlo_done, TILES)
            step(0, 0, 1, pair_a=0)
            with pe.Fori(0, PAIRS - 1) as i:
                for j in range(NSEG):
                    a = 4 * i + 1 + j
                    step(a, (1 + j) % NSEG, a + 1, pair_n=i + 1 if j == 2 else None,
                         pair_a=i + 1 if j == 3 else None)
            late_step(STEPS - 3, 1, 0)
            late_step(STEPS - 2, 2, 1)

            def ffn_unit(narrow, m, seg, u, new_group=None, psum=ffn_ps):
                t, up = u // 2, u % 2
                if new_group is not None and up == 0:
                    pe.wait_ge(flo_done, 2 * new_group + t + 1)
                wait(pe, hid_done, 2 * (m - 1) + t + 1)
                split_product(psum[u][:, :],
                              [(f_hi[:, t, up, r], f_lo[:, t, up, r]) for r in range(HT)],
                              [(x_hi[:, r, tokens(seg)], x_lo[:, r, tokens(seg)]) for r in range(HT)],
                              fproj_done, "stationary" if narrow else None)

            def project_down(narrow, d, par, t, new_group=None):
                if t == 0:
                    pe.wait_ge(hlo_done, 2 * d + 2)
                    if new_group is not None:
                        pe.wait_ge(dlo_done, new_group + 1)
                if isinstance(d, int) and d == 0:
                    pe.wait_ge(yacc_done, 4 * STEPS)
                wait(pe, y2acc_done, 4 * d + t - 1)
                split_product(yp[t % 2][:, :],
                              [(h_hi[par][:, f, chunk(t)], h_lo[par][:, f, chunk(t)]) for f in range(2)],
                              [(d_hi[:, f], d_lo[:, f]) for f in range(2)],
                              down_done, "moving" if narrow else None)

            def ffn_step(narrow, m, seg, d, par, new_group=None, down_group=None):
                for t in range(2):
                    for u in range(2):
                        ffn_unit(narrow, m, seg, 2 * t + u, new_group)
                    for u in range(2):
                        project_down(narrow, d, par, 2 * t + u, down_group)

            def last_step_and_ffn(narrow):
                def project(m, t, psum=ffn_ps):
                    for u in range(2):
                        ffn_unit(narrow, m, m % NSEG, 2 * t + u, 0 if m == 0 else None, psum)

                def down(d):
                    for t in range(CH):
                        project_down(narrow, d, d % 2, t, 0 if d == 0 else None)

                last = STEPS - 1
                pe.wait_ge(xlo_done, TILES + 2 * CH)
                transposes_and_scores(last, 0)
                sums_of_squares(2, yp[0])
                pe.wait_ge(sig_done, 8 * STEPS)
                project(0, 0, ffn_ps_first)
                transposes_and_scores(last, 1)
                contributions(last, 1, 0)
                contributions(last, 1, 1)
                pe.wait_ge(rms_ready, 3)
                pe.wait_ge(yacc_done, 4 * last)
                project(0, 1, ffn_ps_first)
                attend(last, 1, 0)
                attend(last, 1, 1)
                project(1, 0)
                sums_of_squares(3, sc_st[0])
                pe.wait_ge(gated_done, 2 * STEPS)
                project(1, 1)
                pe.wait_ge(hid_done, 2)
                for t in range(CH):
                    project_out(last, t)
                pe.wait_ge(rms_ready, NSEG)
                mid_transposes(2, (0, 1))
                down(0)
                mid_transposes(2, (2, 3))
                pe.wait_ge(xlo_done, TILES + 3 * CH)
                project(2, 0)
                project(2, 1)
                down(1)
                mid_transposes(3, range(CH))
                pe.wait_ge(xlo_done, 2 * TILES)
                project(3, 0)
                project(3, 1)
                down(2)
                with pe.Fori(1, FG - 1) as i:
                    for j in range(NSEG):
                        m = 4 * i + j
                        ffn_step(narrow, m, j, m - 1, (j + 1) % 2,
                                 new_group=i if j == 0 else None, down_group=i if j == 1 else None)
                for j in range(NSEG - 1):
                    m = FSTEPS - NSEG + j
                    ffn_step(narrow, m, j, m - 1, (j + 1) % 2,
                             new_group=FG - 1 if j == 0 else None,
                             down_group=FG - 1 if j == 1 else None)
                project(FSTEPS - 1, 0)
                project(FSTEPS - 1, 1)
                down(FSTEPS - 2)
                down(FSTEPS - 1)

            pe.wait_ge(wide_ready, 1)
            needs_lo = pe.value_load(wide[0:1, 0:1], min_val=0, max_val=1)
            with pe.If(needs_lo == 1):
                last_step_and_ffn(False)
            with pe.Else():
                last_step_and_ffn(True)


def decay_tables(np):
    layer, layers = 1, 32
    base = np.float32(1.0 / 2.0 ** (8.0 / HEADS))
    factor = np.float32(1.0 - layer / (layers - 1 + 1e-05) + 1e-05)
    slope = (base ** (np.arange(HEADS, dtype=np.float32) + np.float32(1)) * factor).astype(np.float32)
    r = np.arange(P, dtype=np.float32) + np.float32(1)
    t = np.zeros((PAIRS, P, TAB), np.float32)
    for head in range(HEADS):
        p, h, s = head // 2, head % 2, slope[head]
        diff = r[None, :] - r[:, None]
        t[p, :, TAB_D + h * P:TAB_D + (h + 1) * P] = np.where(diff >= 0, np.exp(-s * np.abs(diff)), 0)
        t[p, :, TAB_Q + h * P:TAB_Q + (h + 1) * P] = np.exp(-s * r)[None, :]
        t[p, :, TAB_K + h] = np.exp(-s * (np.float32(P) - r))
        t[p, :, TAB_B + h] = np.exp(-s * np.float32(P))
    return t


def kernel(L0_attn_hidden_states, L0_attn_qkv_w, L0_attn_out_w, L0_attn_gate_w, L0_attn_norm_w,
           L0_ffn_gate_t, L0_ffn_up_t, L0_ffn_down_t, L0_ffn_gate_s, L0_ffn_up_s, L0_ffn_down_s):
    import numpy as np
    import concourse.bacc as bacc
    from concourse.bass_utils import run_bass_kernel_spmd

    qkv = np.asarray(L0_attn_qkv_w).reshape(PAIRS, 2, 3, HD, HT, P)
    gate = np.asarray(L0_attn_gate_w).reshape(PAIRS, 2, 1, HD, HT, P)
    w = np.concatenate([qkv[:, :, 1:2], qkv[:, :, 0:1], qkv[:, :, 2:3], gate], axis=2)
    w_attn = w.transpose(0, 2, 5, 4, 1, 3)
    w_out = np.asarray(L0_attn_out_w).reshape(HID, PAIRS, 2, HD).transpose(1, 3, 2, 0)
    norm_w = np.asarray(L0_attn_norm_w).reshape(PAIRS, 2, HD).transpose(0, 2, 1)
    gu = np.stack([np.asarray(L0_ffn_gate_t), np.asarray(L0_ffn_up_t)]).reshape(2, FG, 2, P, HT, P)
    w_ffn = gu.transpose(1, 5, 2, 0, 4, 3)
    w_down = np.asarray(L0_ffn_down_t).reshape(HID, FG, 2, P).transpose(1, 3, 2, 0)
    scales = np.stack([np.asarray(L0_ffn_gate_s), np.asarray(L0_ffn_up_s)]).reshape(2, FG, 2, P)
    arrays = {
        "x": np.asarray(L0_attn_hidden_states).reshape(TOK, HID),
        "w_attn": w_attn, "w_out": w_out, "norm_w": norm_w, "tables": decay_tables(np),
        "w_ints": np.concatenate([w_ffn.ravel(), w_down.ravel()]),
        "ffn_scales": scales.transpose(1, 3, 0, 2).reshape(FG, P, 4),
        "down_s": np.asarray(L0_ffn_down_s),
    }
    arrays = {name: np.ascontiguousarray(a) for name, a in arrays.items()}
    nc = bacc.Bacc("TRN2", target_bir_lowering=False, num_devices=1)
    aps = [nc.dram_tensor(name, a.shape, mybir.dt.from_np(a.dtype), kind="ExternalInput").ap()
           for name, a in arrays.items()]
    out = nc.dram_tensor("out", (TOK, HID), F32, kind="ExternalOutput").ap()
    sandwich_kernel(nc, *aps, out)
    result = run_bass_kernel_spmd(nc, [arrays], core_ids=[0])
    return result.results[0]["out"].reshape(BATCH, SEQ, HID)
```

```python
from contextlib import ExitStack

import concourse.bass as bass
from concourse import mybir
from concourse.alu_op_type import AluOpType as ALU

P = 128
BATCH, SEQ, HID = 2, 1024, 512
TOK = BATCH * SEQ
HEADS, HD = 32, 128
FF = 1792
LN_EPS = 1e-5
RMS_EPS = 1e-5

SEG = 512
NSEG = TOK // SEG
SEGS_PER_BATCH = SEQ // SEG
CH = SEG // P
TILES = TOK // P
HT = HID // P
PAIRS = HEADS // 2
STEPS = PAIRS * NSEG
KK, QQ, VV, GG = range(4)
TAB_D, TAB_Q, TAB_K, TAB_B = 0, 2 * P, 4 * P, 4 * P + 2
TAB = 4 * P + 4

FG = FF // (2 * P)
FSTEPS = FG * NSEG
GU_INTS = 2 * FF * HID
WIDTH_CHECKS = 3 * FF * HID // (P * HID)
CHECKS_PER_PAIR = 3
CHECK_PAIRS = WIDTH_CHECKS // CHECKS_PER_PAIR
F32R_EXACT = 2.0 ** 12

ACT = mybir.ActivationFunctionType
AX = mybir.AxisListType
F32 = mybir.dt.float32
F32R = mybir.dt.float32r
I32 = mybir.dt.int32


def wait(eng, sem, value):
    if isinstance(value, int) and value <= 0:
        return
    eng.wait_ge(sem, value)


def states_before(a, odd):
    return 7 * a + (1 if odd else 0)


def sandwich_kernel(nc, x, w_attn, w_out, norm_w, tables, w_ints, ffn_scales, down_s, out):
    ctx = ExitStack()
    with ctx:
        def sem(name):
            return ctx.enter_context(nc.semaphore(name))

        def sb(name, shape, dt=F32, scope=ctx):
            return scope.enter_context(nc.sbuf_tensor(name, shape, dt))

        one = ExitStack()
        x_hi = sb("x_hi", [P, HT, TOK], F32R, one)
        one.close()
        x_again = sb("x_again", [P, HT, TOK])
        x_lo = sb("x_lo", [P, HT, TOK], F32R)
        y = sb("y", [P, TILES, HID])
        ident = sb("ident", [P, P])
        ones = sb("ones", [P, 1])
        stats = sb("stats", [P, 4, CH, 6])
        meanvar = sb("meanvar", [P, 4, CH, 2])
        var_eps = sb("var_eps", [P, 4, CH])
        stdev = sb("stdev", [P, 4, CH])
        rstd = sb("rstd", [P, 4, CH])
        shift = sb("shift", [P, 4, CH])
        rms_term = sb("rms_term", [P, TILES])
        block_max = sb("block_max", [P, CHECKS_PER_PAIR])
        ints_max = sb("ints_max", [P, CHECKS_PER_PAIR])
        part_max = sb("part_max", [P, 1])
        all_max = sb("all_max", [P, 1])
        wide = sb("wide", [P, 1], I32)
        nw = sb("nw", [P, 2])
        table = sb("table", [P, TAB])
        fs_stage = sb("fs_stage", [P, 4])
        fs = sb("fs", [P, 4])

        def bank(name):
            return ctx.enter_context(nc.psum_tensor(name, [P, SEG], F32))

        proj_ps = [bank("proj_ps0"), bank("proj_ps1")]
        kt_at = [bank("kt_at0"), bank("kt_at1")]
        sc_st = [bank("sc_st0"), bank("sc_st1")]
        yp = [bank("yp0"), bank("yp1")]
        ln1_ring = kt_at + sc_st + yp

        x_in = [sem(f"x_in{s}") for s in range(NSEG)]
        x_first_in = [sem(f"x_first_in{t}") for t in range(CH)]
        raw_in = [sem("raw_in0"), sem("raw_in1")]
        table_in, ow_in, norm_in = sem("table_in"), sem("ow_in"), sem("norm_in")
        const_done = sem("const_done")
        ln_own = sem("ln_own")
        var_ready = sem("var_ready")
        sd_ready = sem("sd_ready")
        scale_ready = sem("scale_ready")
        normed = sem("normed")
        xt_done = sem("xt_done")
        xhi_done = sem("xhi_done")
        xlo_done = sem("xlo_done")
        y_cleared = sem("y_cleared")
        ss_cleared = sem("ss_cleared")
        whi_done = sem("whi_done")
        wlo_done = sem("wlo_done")
        ow_scaled, owhi_done, owlo_done = sem("ow_scaled"), sem("owhi_done"), sem("owlo_done")
        table_ready = sem("table_ready")
        proj_done = sem("proj_done")
        kt_done = sem("kt_done")
        score_done = sem("score_done")
        contrib_done = sem("contrib_done")
        attn_done = sem("attn_done")
        yproj_done = sem("yproj_done")
        sig_done = sem("sig_done")
        kd_done = sem("kd_done")
        sq_done = sem("sq_done")
        ghi_done = sem("ghi_done")
        silu_done = sem("silu_done")
        pdec_done = sem("pdec_done")
        state_done = sem("state_done")
        gated_done = sem("gated_done")
        yacc_done = sem("yacc_done")
        qd_done = sem("qd_done")
        ss_done = sem("ss_done")
        glo_done = sem("glo_done")
        glo_last = sem("glo_last")
        check_in = sem("check_in")
        block_done = sem("block_done")
        max_done = sem("max_done")
        part_done = sem("part_done")
        all_max_done = sem("all_max_done")
        wide_ready = sem("wide_ready")
        ssum_done = sem("ssum_done")
        rms_ready = sem("rms_ready")
        xres_in = [sem(f"xres_in{s}") for s in range(NSEG)]
        mid_added = sem("mid_added")
        ds_in = sem("ds_in")
        fraw_in, draw_in, fs_in = sem("fraw_in"), sem("draw_in"), sem("fs_in")
        fs_ready = sem("fs_ready")
        fcv_done, dcv_done = sem("fcv_done"), sem("dcv_done")
        fhi_done, flo_done = sem("fhi_done"), sem("flo_done")
        dhi_done, dlo_done = sem("dhi_done"), sem("dlo_done")
        fproj_done = sem("fproj_done")
        fsig_done = sem("fsig_done")
        fgate_done = sem("fgate_done")
        hid_done = sem("hid_done")
        hhi_done, hlo_done = sem("hhi_done"), sem("hlo_done")
        down_done = sem("down_done")
        y2_cleared = sem("y2_cleared")
        y2acc_done = sem("y2acc_done")
        final_done = sem("final_done")
        y2_scaled = sem("y2_scaled")
        last_done = sem("last_done")
        out_sent = sem("out_sent")

        two = ExitStack()
        raw = sb("raw", [P, 2, HT, 2, P], scope=two)
        w_hi = sb("w_hi", [P, 4, HT, 2, P], F32R, two)
        w_lo = sb("w_lo", [P, 4, HT, 2, P], F32R, two)
        ow = sb("ow", [P, 2, HID], scope=two)
        check = sb("check", [P, HID], I32, two)
        table_stage = sb("table_stage", [P, TAB], scope=two)
        k = sb("k", [P, 2, SEG], scope=two)
        q = sb("q", [P, 2, SEG], scope=two)
        qd = sb("qd", [P, 2, SEG], scope=two)
        g = sb("g", [P, 2, SEG], scope=two)
        v = sb("v", [P, CH, 2, HD], scope=two)
        kd = sb("kd", [P, 2, CH, HD], scope=two)
        pd = sb("pd", [P, 2, CH, P], scope=two)
        state = sb("state", [P, 2, CH, HD], scope=two)
        g_hi = sb("g_hi", [P, 2, SEG], F32R, two)
        g_lo = sb("g_lo", [P, 2, SEG], F32R, two)
        ow_hi = sb("ow_hi", [P, 2, HID], F32R, two)
        ow_lo = sb("ow_lo", [P, 2, HID], F32R, two)
        sq = sb("sq", [P, 2, SEG], scope=two)
        sumsq = sb("sumsq", [P, TOK], scope=two)
        two.close()

        three = ExitStack()
        fraw = sb("fraw", [P, 2, 2, HT, P], I32, three)
        f_hi = sb("f_hi", [P, 2, 2, HT, P], F32R, three)
        d_hi = sb("d_hi", [P, 2, HID], F32R, three)
        draw = sb("draw", [P, 2, HID], I32, three)
        f_lo = sb("f_lo", [P, 2, 2, HT, P], F32R, three)
        d_lo = sb("d_lo", [P, 2, HID], F32R, three)
        hid = sb("hid", [P, 2, SEG], scope=three)
        xn = sb("xn", [P, CH, HID], scope=three)
        sb("rest_of_stage", [P, TAB - HID], scope=three)
        h_hi = [sb("h_hi0", [P, 2, SEG], F32R, three)]
        h_lo = [sb("h_lo0", [P, 2, SEG], F32R, three)]
        y2 = sb("y2", [P, TILES, HID], scope=three)
        sb("not_used", [P, 2, 2, HID], scope=three)
        ds = sb("ds", [P, 2, HID], scope=three)[:, 0]
        h_hi.append(sb("h_hi1", [P, 2, SEG], F32R, three))
        h_lo.append(sb("h_lo1", [P, 2, SEG], F32R, three))
        three.close()

        xres = [x_again[:, :, s * SEG:(s + 1) * SEG] for s in range(NSEG)]
        ffn_ps = [proj_ps[0], proj_ps[1], kt_at[0], kt_at[1]]
        ffn_ps_first = [proj_ps[0], proj_ps[1], yp[0], yp[1]]
        w_ffn = w_ints[0:GU_INTS].rearrange("(g p t u r f) -> g p t u r f", p=P, t=2, u=2, r=HT, f=P)
        w_down = w_ints[GU_INTS:].rearrange("(g p f n) -> g p f n", p=P, f=2, n=HID)
        w_blocks = w_ints.rearrange("(c p n) -> c p n", p=P, n=HID)
        x_tiles = x.rearrange("(s t p) h -> s p t h", t=CH, p=P)
        out_tiles = out.rearrange("(s t p) h -> s p t h", t=CH, p=P)
        block = ctx.enter_context(nc.Block())

        def tokens(seg):
            return slice(seg * SEG, (seg + 1) * SEG)

        def chunk(c):
            return slice(c * P, (c + 1) * P)

        norm_a = [NSEG + 2 * s for s in range(NSEG)]
        norm_b = [NSEG + 2 * s + 1 for s in range(NSEG)]
        norm_c = [3 * NSEG + s for s in range(NSEG)]

        def normed_count(number, t):
            return CH * number + t + 1

        @block.sync
        def _(sp):
            def attn_weights(p, kind):
                wait(sp, wlo_done, 4 * p + kind - 1)
                sp.dma_start(raw[:, kind % 2], w_attn[p, kind]).then_inc(raw_in[kind % 2], 16)

            def pair_tables(p):
                wait(sp, table_ready, p)
                sp.dma_start(table_stage[:, :], tables[p]).then_inc(table_in, 16)

            def pair_out_weights(p):
                wait(sp, owlo_done, p)
                sp.dma_start(ow[:, :, :], w_out[p]).then_inc(ow_in, 16)
                sp.dma_start(nw[:, :], norm_w[p]).then_inc(norm_in, 16)

            for t in range(CH):
                sp.dma_start(y[:, t], x_tiles[0, :, t]).then_inc(x_first_in[t], 16)
            attn_weights(0, KK)
            for s in range(1, NSEG):
                sp.dma_start(y[:, s * CH:(s + 1) * CH], x_tiles[s]).then_inc(x_in[s], 16)
                if s == 1:
                    attn_weights(0, QQ)
            attn_weights(0, VV)
            attn_weights(0, GG)
            pair_tables(0)
            pair_out_weights(0)
            with sp.Fori(1, PAIRS) as p:
                attn_weights(p, KK)
                attn_weights(p, QQ)
                pair_tables(p)
                pair_out_weights(p)
                attn_weights(p, VV)
                attn_weights(p, GG)

            def ffn_weights(n):
                wait(sp, flo_done, 2 * n)
                sp.dma_start(fraw[:, :, :, :, :], w_ffn[n]).then_inc(fraw_in, 16)
                wait(sp, fs_ready, n)
                sp.dma_start(fs_stage[:, :], ffn_scales[n]).then_inc(fs_in, 16)
                wait(sp, dlo_done, n)
                sp.dma_start(draw[:, :, :], w_down[n]).then_inc(draw_in, 16)

            sp.wait_ge(wlo_done, 4 * PAIRS)
            sp.dma_start(fraw[:, :, :, :, :], w_ffn[0]).then_inc(fraw_in, 16)
            sp.dma_start(fs_stage[:, :], ffn_scales[0]).then_inc(fs_in, 16)
            for s in range(NSEG):
                sp.wait_ge(proj_done, 8 * (STEPS - NSEG + s + 1))
                sp.dma_start(xres[s], x_tiles[s]).then_inc(xres_in[s], 16)
            sp.dma_start(draw[:, :, :], w_down[0]).then_inc(draw_in, 16)
            sp.wait_ge(ss_done, 2 * STEPS)
            sp.dma_start(ds, down_s.partition_broadcast(P)).then_inc(ds_in, 16)
            with sp.Fori(1, FG) as n:
                ffn_weights(n)
            for s in range(2):
                sp.wait_ge(final_done, CH * (s + 1))
                sp.dma_start(out_tiles[s], y[:, s * CH:(s + 1) * CH]).then_inc(out_sent, 16)
            for t in range(CH):
                sp.wait_ge(final_done, 2 * CH + t + 1)
                sp.dma_start(out_tiles[2, :, t], y[:, 2 * CH + t]).then_inc(out_sent, 16)
            for t in range(CH):
                sp.wait_ge(last_done, t + 1)
                sp.dma_start(out_tiles[3, :, t], y[:, 3 * CH + t]).then_inc(out_sent, 16)
            sp.wait_ge(out_sent, 16 * (2 + 2 * CH))

        @block.gpsimd
        def _(pool):
            def split_lo(p, kind):
                pool.wait_ge(whi_done, 4 * p + kind + 1)
                pool.tensor_tensor(w_lo[:, kind], raw[:, kind % 2], w_hi[:, kind].bitcast(F32),
                                   ALU.subtract).then_inc(wlo_done, 1)

            def split_out_lo(p):
                pool.wait_ge(owhi_done, p + 1)
                pool.tensor_tensor(ow_lo[:, :, :], ow[:, :, :], ow_hi[:, :, :].bitcast(F32),
                                   ALU.subtract).then_inc(owlo_done, 1)

            def query_decay(a):
                for h in range(2):
                    pool.wait_ge(silu_done, 6 * a + 3 + h)
                    wait(pool, attn_done, 2 * a + h - 1)
                    decay = table[:, TAB_Q + h * P:TAB_Q + (h + 1) * P]
                    pool.tensor_tensor(qd[:, h].rearrange("p (c n) -> p c n", c=CH),
                                       q[:, h].rearrange("p (c n) -> p c n", c=CH),
                                       decay.unsqueeze(1).to_broadcast([P, CH, P]),
                                       ALU.mult).then_inc(qd_done, 1)

            def add_squares(a, seg):
                for h in range(2):
                    pool.wait_ge(sq_done, 2 * a + h + 1)
                    wait(pool, ss_done, 2 * a + h)
                    pool.tensor_tensor(sumsq[:, tokens(seg)], sumsq[:, tokens(seg)], sq[:, h],
                                       ALU.add).then_inc(ss_done, 1)

            def gated_lo(a):
                for h in range(2):
                    pool.wait_ge(ghi_done, 2 * a + h + 1)
                    pool.tensor_tensor(g_lo[:, h], g[:, h], g_hi[:, h].bitcast(F32),
                                       ALU.subtract).then_inc(glo_done, 1)

            def attention(a, seg):
                query_decay(a)
                add_squares(a, seg)
                gated_lo(a)

            pool.memset(ident[:, :], 0.0).then_inc(const_done, 1)
            pool.wait_ge(const_done, 1)
            pool.affine_select(out=ident[:, :], in_=ident[:, :], compare_op=ALU.not_equal, fill=1.0,
                               base=0, pattern=[[-1, P]], channel_multiplier=1).then_inc(const_done, 1)
            pool.memset(ones[:, :], 1.0).then_inc(const_done, 1)
            pool.memset(sumsq[:, :], 0.0).then_inc(ss_cleared, 1)
            for kind in range(4):
                split_lo(0, kind)
            for s in range(NSEG):
                pool.wait_ge(xt_done, CH * (s + 1))
                pool.memset(y[:, s * CH:(s + 1) * CH].rearrange("p t h -> p (t h)"), 0.0)\
                    .then_inc(y_cleared, 1)
            pool.wait_ge(ss_cleared, 1)
            pool.wait_ge(table_ready, 1)
            attention(0, 0)
            split_out_lo(0)
            with pool.Fori(0, PAIRS - 1) as i:
                for j in range(NSEG):
                    a = 4 * i + 1 + j
                    if j == 3:
                        pool.wait_ge(table_ready, i + 2)
                    attention(a, (1 + j) % NSEG)
                    if j == 1:
                        for kind in range(4):
                            split_lo(i + 1, kind)
                    if j == 3:
                        split_out_lo(i + 1)

            def add_residual(s):
                pool.wait_ge(xres_in[s], 16)
                for t in range(CH):
                    tile = s * CH + t
                    pool.wait_ge(normed, normed_count(norm_a[s], t))
                    pool.tensor_tensor(y[:, tile], y[:, tile], xres[s][:, t],
                                       ALU.add).then_inc(mid_added, 1)

            def ffn_split_lo(n, t):
                pool.wait_ge(fhi_done, 2 * n + t + 1)
                pool.tensor_tensor(f_lo[:, t], fraw[:, t].bitcast(F32), f_hi[:, t].bitcast(F32),
                                   ALU.subtract).then_inc(flo_done, 1)

            def down_split_lo(n):
                pool.wait_ge(dhi_done, n + 1)
                pool.tensor_tensor(d_lo[:, :, :], draw[:, :, :].bitcast(F32),
                                   d_hi[:, :, :].bitcast(F32), ALU.subtract).then_inc(dlo_done, 1)

            def hidden_lo(m, par, t):
                pool.wait_ge(hhi_done, 2 * m + t + 1)
                pool.tensor_tensor(h_lo[par][:, t], hid[:, t], h_hi[par][:, t].bitcast(F32),
                                   ALU.subtract).then_inc(hlo_done, 1)

            def hidden(m, par, split=None):
                for t in range(2):
                    if split is not None:
                        ffn_split_lo(split, t)
                    hidden_lo(m, par, t)

            def last_residual(s):
                for t in range(CH):
                    tile = s * CH + t
                    pool.wait_ge(normed, normed_count(norm_c[s], t))
                    pool.tensor_tensor(y[:, tile], y[:, tile], y2[:, tile],
                                       ALU.add).then_inc(final_done, 1)

            pool.wait_ge(part_done, 1)
            pool.partition_all_reduce(all_max[:, :], part_max[:, :], P,
                                      bass.bass_isa.ReduceOp.max).then_inc(all_max_done, 1)
            query_decay(STEPS - 3)
            add_residual(0)
            add_squares(STEPS - 3, 1)
            gated_lo(STEPS - 3)
            query_decay(STEPS - 2)
            add_residual(1)
            ffn_split_lo(0, 0)
            add_squares(STEPS - 2, 2)
            gated_lo(STEPS - 2)
            ffn_split_lo(0, 1)
            query_decay(STEPS - 1)
            pool.wait_ge(qd_done, 2 * STEPS)
            hidden_lo(0, 0, 0)
            add_residual(2)
            add_squares(STEPS - 1, 3)
            hidden_lo(0, 0, 1)
            down_split_lo(0)
            hidden(1, 1)
            add_residual(3)
            hidden(2, 0)
            pool.wait_ge(yacc_done, 4 * STEPS)
            pool.memset(y2[:, 3 * CH:].rearrange("p t h -> p (t h)"), 0.0).then_inc(y2_cleared, 1)
            hidden(3, 1, split=1)
            with pool.Fori(1, FG - 1) as i:
                for j in range(NSEG):
                    if j == 1:
                        down_split_lo(i)
                    hidden(4 * i + j, j % 2, split=i + 1 if j == 3 else None)
            for j in range(NSEG):
                if j == 1:
                    down_split_lo(FG - 1)
                hidden(FSTEPS - NSEG + j, j % 2)
            for t in range(CH):
                pool.wait_ge(y2acc_done, NSEG * CH * (FG - 1) + 2 * CH + t + 1)
                pool.tensor_tensor(y2[:, 2 * CH + t], y2[:, 2 * CH + t], ds,
                                   ALU.mult).then_inc(y2_scaled, 1)
            last_residual(0)
            last_residual(1)
            last_residual(2)

        @block.scalar
        def _(act):
            def square_root(number):
                act.wait_ge(var_ready, number + 1)
                act.activation(stdev[:, number % 4], var_eps[:, number % 4],
                               ACT.Sqrt).then_inc(sd_ready, 1)

            def normalise(src, dst, number, tiles=range(CH)):
                act.wait_ge(scale_ready, number + 1)
                for t in tiles:
                    act.activation(dst(t), src(t), ACT.Identity,
                                   bias=shift[:, number % 4, t:t + 1],
                                   scale=rstd[:, number % 4, t:t + 1]).then_inc(normed, 1)

            def x_hi_part(t, psum, count):
                act.wait_ge(xt_done, count + 1)
                act.activation(x_hi[:, :, chunk(t)], psum[:, :].rearrange("p (h n) -> p h n", h=HT),
                               ACT.Copy).then_inc(xhi_done, 1)

            def split_hi(p, kind, n):
                act.wait_ge(raw_in[kind % 2], 32 * p + 16 * (kind // 2) + 16)
                if n is not None:
                    act.wait_ge(proj_done, 8 * n + (2, 4, 6, 8)[kind])
                act.activation(w_hi[:, kind], raw[:, kind % 2], ACT.Copy).then_inc(whi_done, 1)

            def split_out_hi(p, a):
                act.wait_ge(ow_scaled, 2 * p + 2)
                wait(act, yproj_done, 4 * a)
                act.activation(ow_hi[:, :, :], ow[:, :, :], ACT.Copy).then_inc(owhi_done, 1)

            def sigmoid(n, u):
                act.wait_ge(proj_done, 8 * n + u + 1)
                a = n - 1
                h = u % 2
                if u < 2:
                    wait(act, score_done, 2 * a + h + 1)
                    dst, src = k[:, h], proj_ps[h][:, :]
                elif u < 4:
                    wait(act, score_done, 2 * a + h + 1)
                    wait(act, qd_done, 2 * a + h + 1)
                    dst, src = q[:, h], proj_ps[h][:, :]
                elif u < 6:
                    wait(act, attn_done, 2 * a + 2)
                    dst = v[:, 2 * h:2 * h + 2].rearrange("p c h d -> p (c h d)")
                    src = proj_ps[h][:, :]
                else:
                    wait(act, glo_done, 2 * a + h + 1)
                    dst, src = g[:, h], proj_ps[h][:, :]
                act.activation(dst, src, ACT.Sigmoid).then_inc(sig_done, 1)

            def k_decay(a, h):
                act.wait_ge(kt_done, 2 * a + h + 1)
                wait(act, contrib_done, 2 * a + h - 1)
                act.activation(kd[:, h].rearrange("p c d -> p (c d)"), kt_at[h][:, :], ACT.Copy,
                               scale=table[:, TAB_K + h:TAB_K + h + 1]).then_inc(kd_done, 1)

            def square(a, h):
                act.wait_ge(attn_done, 2 * a + h + 1)
                wait(act, ss_done, 2 * a + h - 1)
                act.activation(sq[:, h], kt_at[h][:, :], ACT.Square).then_inc(sq_done, 1)

            def gated_hi(a, h):
                act.wait_ge(gated_done, 2 * a + h + 1)
                wait(act, yproj_done, 4 * a)
                act.activation(g_hi[:, h], g[:, h], ACT.Copy).then_inc(ghi_done, 1)

            def step(a, n, table_count=None, split=None, out_split=None):
                if table_count is not None:
                    act.wait_ge(table_ready, table_count)
                for h in range(2):
                    k_decay(a, h)
                    sigmoid(n, h)
                sigmoid(n, 2)
                sigmoid(n, 3)
                square(a, 0)
                square(a, 1)
                if out_split is not None:
                    split_out_hi(out_split, a)
                gated_hi(a, 0)
                gated_hi(a, 1)
                for u in range(4, 8):
                    sigmoid(n, u)
                    if split is not None:
                        split_hi(split, (KK, QQ, VV, GG)[u - 4], n)

            def y_tile(s):
                return lambda t: y[:, s * CH + t]

            square_root(0)
            normalise(y_tile(0), y_tile(0), 0)
            for t in range(CH):
                x_hi_part(t, ln1_ring[t % 6], t)
            act.wait_ge(wlo_done, 1)
            split_hi(0, QQ, None)
            square_root(1)
            normalise(y_tile(1), y_tile(1), 1)
            square_root(2)
            for s in range(1, NSEG):
                sigmoid(0, 2 * s - 2)
                sigmoid(0, 2 * s - 1)
                for t in range(s * CH, (s + 1) * CH):
                    x_hi_part(t, ln1_ring[t % 6], t)
                if s < NSEG - 1:
                    normalise(y_tile(s + 1), y_tile(s + 1), s + 1)
                    split_hi(0, (VV, GG)[s - 1], None)
                if s == 1:
                    square_root(3)
            sigmoid(0, 6)
            sigmoid(0, 7)

            def four_steps(i, checks):
                for j in range(NSEG):
                    a = 4 * i + 1 + j
                    if checks and j < CHECKS_PER_PAIR:
                        c = CHECKS_PER_PAIR * i + j
                        act.wait_ge(max_done, c + 1)
                        act.dma_start(check[:, :], w_blocks[c]).then_inc(check_in, 16)
                    step(a, a + 1, table_count=i + 2 if j == 3 else None,
                         split=i + 1 if j == 1 else None, out_split=i + 1 if j == 3 else None)

            step(0, 1, table_count=1, out_split=0)
            with act.Fori(0, CHECK_PAIRS) as i:
                four_steps(i, True)
            with act.Fori(CHECK_PAIRS, PAIRS - 1) as i:
                four_steps(i, False)

            def normalise_a(s, tiles=range(CH)):
                normalise(y_tile(s), y_tile(s), norm_a[s], tiles)

            def normalise_b(s, tiles):
                if s > 0:
                    act.wait_ge(xt_done, TILES + CH * s)
                normalise(y_tile(s), lambda t: xn[:, t], norm_b[s], tiles)

            def mid_hi(s, tiles):
                for t in tiles:
                    x_hi_part(s * CH + t, sc_st[t % 2], TILES + s * CH + t)

            def ffn_convert(n):
                act.wait_ge(fraw_in, 16 * (n + 1))
                act.activation(fraw[:, :].bitcast(F32), fraw[:, :], ACT.Copy).then_inc(fcv_done, 1)

            def ffn_split_hi(n, t, m):
                act.wait_ge(fcv_done, n + 1)
                if m is not None:
                    act.wait_ge(fproj_done, 4 * m + 2 * t + 2)
                else:
                    act.wait_ge(proj_done, 8 * (STEPS - 1) + 2 * t + 2)
                act.activation(f_hi[:, t], fraw[:, t].bitcast(F32), ACT.Copy).then_inc(fhi_done, 1)

            def down_split_hi(n, d):
                act.wait_ge(draw_in, 16 * (n + 1))
                act.activation(draw[:, :, :].bitcast(F32), draw[:, :, :], ACT.Copy)\
                    .then_inc(dcv_done, 1)
                act.wait_ge(dcv_done, n + 1)
                wait(act, down_done, 4 * d)
                act.activation(d_hi[:, :, :], draw[:, :, :].bitcast(F32), ACT.Copy)\
                    .then_inc(dhi_done, 1)

            def ffn_sigmoid(m, t, psum=ffn_ps):
                act.wait_ge(fproj_done, 4 * m + 2 * t + 1)
                wait(act, hlo_done, 2 * m + t - 1)
                act.activation(hid[:, t], psum[2 * t][:, :], ACT.Sigmoid,
                               scale=fs[:, t:t + 1]).then_inc(fsig_done, 1)

            def hidden_hi(m, par, t):
                act.wait_ge(hid_done, 2 * m + t + 1)
                wait(act, down_done, 4 * (m - 1))
                act.activation(h_hi[par][:, t], hid[:, t], ACT.Copy).then_inc(hhi_done, 1)

            def late_step(a, s):
                n = a + 1
                k_decay(a, 0)
                sigmoid(n, 0)
                k_decay(a, 1)
                sigmoid(n, 1)
                square_root(norm_a[s])
                normalise_a(s)
                sigmoid(n, 2)
                if n == STEPS - 1:
                    ffn_convert(0)
                    ffn_split_hi(0, 0, None)
                sigmoid(n, 3)
                square(a, 0)
                square(a, 1)
                square_root(norm_b[s])
                gated_hi(a, 0)
                gated_hi(a, 1)
                sigmoid(n, 4)
                normalise_b(s, (0, 1))
                sigmoid(n, 5)
                normalise_b(s, (2, 3))
                mid_hi(s, (0, 1))
                sigmoid(n, 6)
                mid_hi(s, (2, 3))
                if n == STEPS - 1:
                    ffn_split_hi(0, 1, None)
                sigmoid(n, 7)

            late_step(STEPS - 3, 0)
            late_step(STEPS - 2, 1)
            last = STEPS - 1
            k_decay(last, 0)
            square_root(norm_a[2])
            act.wait_ge(fs_ready, 1)
            ffn_sigmoid(0, 0, ffn_ps_first)
            k_decay(last, 1)
            act.wait_ge(score_done, 2 * STEPS)
            hidden_hi(0, 0, 0)
            normalise_a(2)
            down_split_hi(0, 0)
            ffn_sigmoid(0, 1, ffn_ps_first)
            square(last, 0)
            square(last, 1)
            hidden_hi(0, 0, 1)
            square_root(norm_b[2])
            gated_hi(last, 0)
            gated_hi(last, 1)
            ffn_sigmoid(1, 0)
            normalise_b(2, range(CH))
            act.wait_ge(ssum_done, NSEG)
            hidden_hi(1, 1, 0)
            ffn_sigmoid(1, 1)
            hidden_hi(1, 1, 1)
            mid_hi(2, (0, 1))
            square_root(norm_a[3])
            normalise_a(3, (0, 1))
            mid_hi(2, (2, 3))
            normalise_a(3, (2, 3))
            ffn_sigmoid(2, 0)
            hidden_hi(2, 0, 0)
            ffn_sigmoid(2, 1)
            hidden_hi(2, 0, 1)
            square_root(norm_b[3])
            normalise_b(3, range(CH))
            mid_hi(3, range(CH))
            ffn_convert(1)

            def ffn_step(m, par, scales=None, convert=None, split=None, down=None):
                if scales is not None:
                    act.wait_ge(fs_ready, scales)
                if down is not None:
                    down_split_hi(down, m - 1)
                for t in range(2):
                    ffn_sigmoid(m, t)
                    if split is not None:
                        ffn_split_hi(split, t, m)
                    hidden_hi(m, par, t)
                if convert is not None:
                    ffn_convert(convert)

            ffn_step(3, 1, split=1)
            with act.Fori(1, FG - 1) as i:
                for j in range(NSEG):
                    ffn_step(4 * i + j, j % 2, scales=i + 1 if j == 0 else None,
                             convert=i + 1 if j == 2 else None,
                             split=i + 1 if j == 3 else None, down=i if j == 1 else None)

            def final_norm(s):
                square_root(norm_c[s])
                normalise(lambda t: y2[:, s * CH + t], lambda t: y2[:, s * CH + t], norm_c[s])

            for j in range(NSEG):
                ffn_step(FSTEPS - NSEG + j, j % 2, scales=FG if j == 0 else None,
                         down=FG - 1 if j == 1 else None)
            for s in range(NSEG - 1):
                final_norm(s)
            square_root(norm_c[3])

        @block.vector
        def _(dve):
            own = [0]

            def tile_statistics(src, number, t):
                dve.bn_stats(stats[:, number % 4, t], src(t)).then_inc(ln_own, 1)
                own[0] += 1

            def norm_variances(number, extra=None):
                z = number % 4
                dve.wait_ge(ln_own, own[0])
                for t in range(CH):
                    dve.bn_aggr(meanvar[:, z, t], stats[:, z, t]).then_inc(ln_own, 1)
                own[0] += CH
                dve.wait_ge(ln_own, own[0])
                if extra is None:
                    dve.tensor_scalar(var_eps[:, z], meanvar[:, z, :, 1], LN_EPS, None,
                                      ALU.add).then_inc(var_ready, 1)
                else:
                    dve.tensor_tensor(var_eps[:, z], meanvar[:, z, :, 1], extra,
                                      ALU.add).then_inc(var_ready, 1)

            def norm_statistics(src, number):
                for t in range(CH):
                    tile_statistics(src, number, t)
                norm_variances(number)

            def norm_scales(number):
                z = number % 4
                dve.wait_ge(sd_ready, number + 1)
                dve.reciprocal(rstd[:, z], stdev[:, z]).then_inc(ln_own, 1)
                own[0] += 1
                dve.wait_ge(ln_own, own[0])
                dve.scalar_tensor_tensor(shift[:, z], meanvar[:, z, :, 0], -1.0, rstd[:, z],
                                         ALU.mult, ALU.mult).then_inc(scale_ready, 1)

            def x_lo_part(t, psum, count):
                dve.wait_ge(xhi_done, count + 1)
                dve.tensor_tensor(x_lo[:, :, chunk(t)], psum[:, :].rearrange("p (h n) -> p h n", h=HT),
                                  x_hi[:, :, chunk(t)].bitcast(F32), ALU.subtract).then_inc(xlo_done, 1)

            def next_table(a, p):
                wait(dve, kd_done, 2 * a)
                wait(dve, qd_done, 2 * a)
                dve.wait_ge(table_in, 16 * (p + 1))
                dve.tensor_copy(table[:, :], table_stage[:, :]).then_inc(table_ready, 1)
                dve.wait_ge(table_ready, p + 1)

            def scale_out_weights(p):
                dve.wait_ge(ow_in, 16 * (p + 1))
                dve.wait_ge(norm_in, 16 * (p + 1))
                for h in range(2):
                    dve.tensor_scalar(ow[:, h], ow[:, h], nw[:, h:h + 1], None,
                                      ALU.mult).then_inc(ow_scaled, 1)

            def silu(n, u):
                dve.wait_ge(sig_done, 8 * n + u + 1)
                h = u % 2
                dst = (k[:, h], q[:, h], v[:, 2 * h:2 * h + 2].rearrange("p c h d -> p (c h d)"))[u // 2]
                dve.tensor_tensor(dst, proj_ps[h][:, :], dst, ALU.mult).then_inc(silu_done, 1)

            def decay_scores(a, h):
                dve.wait_ge(score_done, 2 * a + h + 1)
                wait(dve, attn_done, 2 * a + h - 1)
                mask = table[:, TAB_D + h * P:TAB_D + (h + 1) * P]
                dve.tensor_tensor(pd[:, h], sc_st[h][:, :].rearrange("p (c n) -> p c n", c=CH),
                                  mask.unsqueeze(1).to_broadcast([P, CH, P]),
                                  ALU.mult).then_inc(pdec_done, 1)

            def update_state(a, odd, h):
                dve.wait_ge(contrib_done, 2 * a + h + 1)
                done = states_before(a, odd) + h * (CH - odd)
                for c in range(CH - odd):
                    new = sc_st[h][:, chunk(c)]
                    if c == 0 and not odd:
                        dve.tensor_copy(state[:, h, 0], new).then_inc(state_done, 1)
                        continue
                    wait(dve, state_done, done + c)
                    dve.scalar_tensor_tensor(state[:, h, c], state[:, h, (c - 1) % CH],
                                             table[:, TAB_B + h:TAB_B + h + 1], new,
                                             ALU.mult, ALU.add).then_inc(state_done, 1)

            def gate(a, h):
                dve.wait_ge(sq_done, 2 * a + h + 1)
                dve.wait_ge(sig_done, 8 * a + 7 + h)
                dve.tensor_tensor(g[:, h], kt_at[h][:, :], g[:, h], ALU.mult).then_inc(gated_done, 1)

            def add_out(a, seg, t):
                dve.wait_ge(yproj_done, 4 * a + t + 1)
                tile = y[:, seg * CH + t]
                dve.tensor_tensor(tile, yp[t % 2][:, :], tile, ALU.add).then_inc(yacc_done, 1)

            def step(a, seg, n, pair=None):
                odd = seg % 2
                if pair is not None:
                    next_table(a, pair)
                for h in range(2):
                    decay_scores(a, h)
                    silu(n, h)
                update_state(a, odd, 0)
                update_state(a, odd, 1)
                silu(n, 2)
                silu(n, 3)
                if pair is not None:
                    scale_out_weights(pair)
                gate(a, 0)
                gate(a, 1)
                silu(n, 4)
                silu(n, 5)
                for t in range(CH):
                    add_out(a, seg, t)

            def y_tile(s):
                return lambda t: y[:, s * CH + t]

            for t in range(CH):
                dve.wait_ge(x_first_in[t], 16)
                tile_statistics(y_tile(0), 0, t)
            norm_variances(0)
            norm_scales(0)
            dve.wait_ge(raw_in[0], 16)
            dve.tensor_copy(w_hi[:, KK], raw[:, 0]).then_inc(whi_done, 1)
            for t in range(CH):
                x_lo_part(t, ln1_ring[t % 6], t)
            for s in (1, 2):
                dve.wait_ge(x_in[s], 16)
                norm_statistics(y_tile(s), s)
                norm_scales(s)
            for s in range(1, NSEG):
                silu(0, 2 * s - 2)
                silu(0, 2 * s - 1)
                if s == 1:
                    dve.wait_ge(x_in[3], 16)
                    norm_statistics(y_tile(3), 3)
                for t in range(s * CH, (s + 1) * CH):
                    x_lo_part(t, ln1_ring[t % 6], t)
                if s == 1:
                    norm_scales(3)

            def look_at_block(c, j):
                dve.wait_ge(check_in, 16 * (c + 1))
                dve.wait_ge(max_done, c + 1)
                dve.tensor_reduce(block_max[:, j:j + 1], check[:, :], AX.X, ALU.max,
                                  apply_absolute_value=True).then_inc(block_done, 1)
                dve.wait_ge(block_done, c + 1)
                dve.tensor_tensor(ints_max[:, j:j + 1], ints_max[:, j:j + 1], block_max[:, j:j + 1],
                                  ALU.max).then_inc(max_done, 1)

            def four_steps(i, checks):
                for j in range(NSEG):
                    a = 4 * i + 1 + j
                    step(a, (1 + j) % NSEG, a + 1, pair=i + 1 if j == 3 else None)
                    if checks and j < CHECKS_PER_PAIR:
                        look_at_block(CHECKS_PER_PAIR * i + j, j)

            dve.memset(ints_max[:, :], 0.0).then_inc(max_done, 1)
            dve.wait_ge(y_cleared, 1)
            step(0, 0, 1, pair=0)
            dve.wait_ge(y_cleared, NSEG)
            with dve.Fori(0, CHECK_PAIRS) as i:
                four_steps(i, True)
            dve.wait_ge(max_done, WIDTH_CHECKS + 1)
            dve.tensor_reduce(part_max[:, :], ints_max[:, :], AX.X, ALU.max).then_inc(part_done, 1)
            with dve.Fori(CHECK_PAIRS, PAIRS - 1) as i:
                four_steps(i, False)
            def rms(s, psum):
                dve.wait_ge(ssum_done, s + 1)
                dve.tensor_scalar(rms_term[:, s * CH:(s + 1) * CH], psum[:, 0:CH],
                                  LN_EPS / (HEADS * HD), LN_EPS * RMS_EPS,
                                  ALU.mult, ALU.add).then_inc(rms_ready, 1)

            def add_out_and_statistics(a, s, tiles=range(CH)):
                for t in tiles:
                    add_out(a, s, t)
                    dve.wait_ge(yacc_done, 4 * a + t + 1)
                    tile_statistics(y_tile(s), norm_a[s], t)

            def variances_a(s):
                dve.wait_ge(rms_ready, s + 1)
                norm_variances(norm_a[s], extra=rms_term[:, s * CH:(s + 1) * CH])

            def statistics_b(s, tiles):
                for t in tiles:
                    dve.wait_ge(mid_added, CH * s + t + 1)
                    tile_statistics(y_tile(s), norm_b[s], t)

            def mid_lo(s, tiles):
                for t in tiles:
                    x_lo_part(s * CH + t, sc_st[t % 2], TILES + s * CH + t)

            def late_step(a, seg, s):
                n = a + 1
                decay_scores(a, 0)
                silu(n, 0)
                rms(s, yp[0])
                variances_a(s)
                decay_scores(a, 1)
                silu(n, 1)
                norm_scales(norm_a[s])
                update_state(a, seg % 2, 0)
                update_state(a, seg % 2, 1)
                statistics_b(s, (0, 1))
                silu(n, 2)
                statistics_b(s, (2, 3))
                norm_variances(norm_b[s])
                silu(n, 3)
                gate(a, 0)
                gate(a, 1)
                norm_scales(norm_b[s])
                silu(n, 4)
                silu(n, 5)
                mid_lo(s, range(CH))
                add_out_and_statistics(a, seg)

            def new_scales(n):
                wait(dve, hid_done, 2 * NSEG * n)
                dve.wait_ge(fs_in, 16 * (n + 1))
                dve.tensor_copy(fs[:, :], fs_stage[:, :]).then_inc(fs_ready, 1)
                dve.wait_ge(fs_ready, n + 1)

            def hidden(m, t, psum=ffn_ps):
                dve.wait_ge(fsig_done, 2 * m + t + 1)
                dve.scalar_tensor_tensor(hid[:, t], psum[2 * t][:, :], fs[:, t:t + 1], hid[:, t],
                                         ALU.mult, ALU.mult).then_inc(fgate_done, 1)
                dve.wait_ge(fproj_done, 4 * m + 2 * t + 2)
                dve.wait_ge(fgate_done, 2 * m + t + 1)
                dve.scalar_tensor_tensor(hid[:, t], psum[2 * t + 1][:, :], fs[:, 2 + t:3 + t],
                                         hid[:, t], ALU.mult, ALU.mult).then_inc(hid_done, 1)

            def add_down(d, seg, t, first=False):
                dve.wait_ge(down_done, 4 * d + t + 1)
                tile = y2[:, seg * CH + t]
                if first:
                    dve.tensor_copy(tile, yp[t % 2][:, :]).then_inc(y2acc_done, 1)
                else:
                    dve.tensor_tensor(tile, yp[t % 2][:, :], tile, ALU.add).then_inc(y2acc_done, 1)

            dve.wait_ge(all_max_done, 1)
            dve.tensor_scalar(wide[:, :], all_max[:, :], F32R_EXACT, None,
                              ALU.is_gt).then_inc(wide_ready, 1)
            dve.wait_ge(yacc_done, 4 * (STEPS - 3))
            for t in range(CH):
                tile_statistics(y_tile(0), norm_a[0], t)
            late_step(STEPS - 3, 1, 0)
            late_step(STEPS - 2, 2, 1)
            last = STEPS - 1
            decay_scores(last, 0)
            new_scales(0)
            rms(2, yp[0])
            variances_a(2)
            norm_scales(norm_a[2])
            decay_scores(last, 1)
            hidden(0, 0, ffn_ps_first)
            update_state(last, 1, 0)
            update_state(last, 1, 1)
            statistics_b(2, (0, 1))
            hidden(0, 1, ffn_ps_first)
            statistics_b(2, (2, 3))
            norm_variances(norm_b[2])
            gate(last, 0)
            gate(last, 1)
            norm_scales(norm_b[2])
            for h in range(2):
                dve.wait_ge(ghi_done, 2 * last + h + 1)
                dve.tensor_tensor(g_lo[:, h], g[:, h], g_hi[:, h].bitcast(F32),
                                  ALU.subtract).then_inc(glo_last, 1)
            hidden(1, 0)
            rms(3, sc_st[0])
            add_out_and_statistics(last, NSEG - 1, (0, 1))
            hidden(1, 1)
            add_out_and_statistics(last, NSEG - 1, (2, 3))
            variances_a(3)
            for t in range(2):
                add_down(0, 0, t, first=True)
            norm_scales(norm_a[3])
            mid_lo(2, (0, 1))
            for t in range(2, CH):
                add_down(0, 0, t, first=True)
            mid_lo(2, (2, 3))
            statistics_b(3, (0, 1))
            hidden(2, 0)
            statistics_b(3, (2, 3))
            norm_variances(norm_b[3])
            hidden(2, 1)
            for t in range(2):
                add_down(1, 1, t, first=True)
            norm_scales(norm_b[3])
            for t in range(2, CH):
                add_down(1, 1, t, first=True)
            for pair in ((0, 1), (2, 3)):
                mid_lo(3, pair)
                for t in pair:
                    add_down(2, 2, t, first=True)
            hidden(3, 0)
            hidden(3, 1)
            dve.wait_ge(y2_cleared, 1)

            def ffn_step(m, d, seg, scales=None):
                if scales is not None:
                    new_scales(scales)
                for t in range(2):
                    hidden(m, t)
                    add_down(d, seg, 2 * t)
                    add_down(d, seg, 2 * t + 1)

            def statistics_c(s, tiles):
                for t in tiles:
                    tile = y2[:, s * CH + t]
                    if s == 2:
                        dve.wait_ge(y2_scaled, t + 1)
                    else:
                        dve.wait_ge(y2acc_done, NSEG * CH * (FG - 1) + CH * s + t + 1)
                        dve.tensor_tensor(tile, tile, ds, ALU.mult).then_inc(ln_own, 1)
                        own[0] += 1
                        dve.wait_ge(ln_own, own[0])
                    tile_statistics(lambda t: y2[:, s * CH + t], norm_c[s], t)

            with dve.Fori(1, FG - 1) as i:
                for j in range(NSEG):
                    m = 4 * i + j
                    ffn_step(m, m - 1, (j - 1) % NSEG, scales=i if j == 0 else None)
            dve.wait_ge(ds_in, 16)
            first = FSTEPS - NSEG
            ffn_step(first, first - 1, 3, scales=FG - 1)
            ffn_step(first + 1, first, 0)
            statistics_c(0, range(CH))
            norm_variances(norm_c[0])
            ffn_step(first + 2, first + 1, 1)
            statistics_c(1, (0, 1))
            hidden(first + 3, 0)
            hidden(first + 3, 1)
            for t in range(CH):
                add_down(first + 2, 2, t)
            norm_scales(norm_c[0])
            statistics_c(1, (2, 3))
            norm_variances(norm_c[1])
            for t in range(2):
                add_down(first + 3, 3, t)
            statistics_c(2, range(CH))
            norm_variances(norm_c[2])
            norm_scales(norm_c[1])
            statistics_c(3, (0, 1))
            norm_scales(norm_c[2])
            for t in range(2, CH):
                add_down(first + 3, 3, t)
                statistics_c(3, (t,))
            norm_variances(norm_c[3])
            norm_scales(norm_c[3])
            dve.wait_ge(scale_ready, norm_c[3] + 1)
            for t in range(CH):
                tile = y2[:, 3 * CH + t]
                dve.tensor_scalar(tile, tile, rstd[:, norm_c[3] % 4, t:t + 1],
                                  shift[:, norm_c[3] % 4, t:t + 1],
                                  ALU.mult, ALU.add).then_inc(ln_own, 1)
                own[0] += 1
                dve.wait_ge(ln_own, own[0])
                dve.tensor_tensor(y[:, 3 * CH + t], y[:, 3 * CH + t], tile,
                                  ALU.add).then_inc(last_done, 1)

        @block.tensor
        def _(pe):
            def split_product(psum, stationary, moving, done=None, drop=None):
                terms = []
                for s, m in zip(stationary, moving):
                    terms.append((s[0], m[0]))
                    if drop != "moving":
                        terms.append((s[0], m[1]))
                    if drop != "stationary":
                        terms.append((s[1], m[0]))
                for n, (s, m) in enumerate(terms):
                    last = pe.matmul(psum, s, m, start=n == 0, stop=n == len(terms) - 1)
                if done is not None:
                    last.then_inc(done, 1)

            def transpose_x(t, src, psum, count):
                pe.wait_ge(normed, count)
                for h in range(HT):
                    last = pe.transpose(psum[:, chunk(h)], src[:, chunk(h)], ident[:, :])
                last.then_inc(xt_done, 1)

            def unit(n, seg, u, new_pair=None):
                if new_pair is not None and u in (0, 2, 4, 6):
                    pe.wait_ge(wlo_done, 4 * new_pair + u // 2 + 1)
                if u < 2:
                    wait(pe, sig_done, 8 * n - 1 + u)
                else:
                    pe.wait_ge(silu_done, 6 * n + u - 1)
                h = u % 2
                if u in (4, 5):
                    for c in range(2):
                        tok = slice(seg * SEG + (2 * h + c) * P, seg * SEG + (2 * h + c + 1) * P)
                        split_product(
                            proj_ps[h][:, c * 2 * HD:(c + 1) * 2 * HD],
                            [(x_hi[:, r, tok], x_lo[:, r, tok]) for r in range(HT)],
                            [(w_hi[:, VV, r].rearrange("p h d -> p (h d)"),
                              w_lo[:, VV, r].rearrange("p h d -> p (h d)")) for r in range(HT)],
                            proj_done if c == 1 else None)
                    return
                kind = (KK, QQ, VV, GG)[u // 2]
                split_product(proj_ps[h][:, :],
                              [(w_hi[:, kind, r, h], w_lo[:, kind, r, h]) for r in range(HT)],
                              [(x_hi[:, r, tokens(seg)], x_lo[:, r, tokens(seg)]) for r in range(HT)],
                              proj_done)

            def transposes_and_scores(a, h):
                pe.wait_ge(silu_done, 6 * a + 3 + h)
                wait(pe, gated_done, 2 * a + h - 1)
                for c in range(CH):
                    last = pe.transpose(kt_at[h][:, chunk(c)], k[:, h, chunk(c)], ident[:, :])
                last.then_inc(kt_done, 1)
                for c in range(CH):
                    last = pe.matmul(sc_st[h][:, chunk(c)], k[:, h, chunk(c)], q[:, h, chunk(c)],
                                     start=True, stop=True)
                last.then_inc(score_done, 1)

            def contributions(a, odd, h):
                pe.wait_ge(silu_done, 6 * a + 6)
                pe.wait_ge(kd_done, 2 * a + h + 1)
                pe.wait_ge(pdec_done, 2 * a + h + 1)
                for c in range(CH - odd):
                    last = pe.matmul(sc_st[h][:, chunk(c)], kd[:, h, c], v[:, c, h],
                                     start=True, stop=True)
                last.then_inc(contrib_done, 1)

            def attend(a, odd, h):
                pe.wait_ge(qd_done, 2 * a + h + 1)
                pe.wait_ge(state_done, states_before(a, odd) + (h + 1) * (CH - odd))
                for c in range(CH):
                    inter = c > 0 or odd
                    last = pe.matmul(kt_at[h][:, chunk(c)], v[:, c, h], pd[:, h, c],
                                     start=True, stop=not inter)
                    if inter:
                        last = pe.matmul(kt_at[h][:, chunk(c)], state[:, h, (c - 1) % CH],
                                         qd[:, h, chunk(c)], start=False, stop=True)
                last.then_inc(attn_done, 1)

            def project_out(a, t, new_pair=None):
                if isinstance(a, int) and a == STEPS - 1:
                    pe.wait_ge(glo_last, 2)
                elif t == 0:
                    pe.wait_ge(glo_done, 2 * a + 2)
                    if new_pair is not None:
                        pe.wait_ge(owlo_done, new_pair + 1)
                wait(pe, yacc_done, 4 * a + t - 1)
                split_product(yp[t % 2][:, :],
                              [(g_hi[:, h, chunk(t)], g_lo[:, h, chunk(t)]) for h in range(2)],
                              [(ow_hi[:, h], ow_lo[:, h]) for h in range(2)],
                              yproj_done)

            def sums_of_squares(s, psum):
                pe.wait_ge(ss_done, 2 * (STEPS - NSEG + s + 1))
                if s < NSEG - 1:
                    pe.wait_ge(yacc_done, 4 * (STEPS - NSEG + s + 1) - 1)
                for t in range(CH):
                    last = pe.matmul(psum[:, t:t + 1], sumsq[:, chunk(s * CH + t)], ones[:, :],
                                     start=True, stop=True)
                last.then_inc(ssum_done, 1)

            def mid_transposes(s, tiles):
                for t in tiles:
                    tile = s * CH + t
                    wait(pe, xlo_done, TILES + tile - 1)
                    transpose_x(tile, xn[:, t], sc_st[t % 2], normed_count(norm_b[s], t))

            def step(a, seg, n, pair_n=None, pair_a=None):
                odd = seg % 2
                seg_n = (seg + 1) % NSEG
                transposes_and_scores(a, 0)
                unit(n, seg_n, 0, pair_n)
                transposes_and_scores(a, 1)
                unit(n, seg_n, 1, pair_n)
                contributions(a, odd, 0)
                contributions(a, odd, 1)
                unit(n, seg_n, 2, pair_n)
                unit(n, seg_n, 3, pair_n)
                attend(a, odd, 0)
                attend(a, odd, 1)
                unit(n, seg_n, 4, pair_n)
                unit(n, seg_n, 5, pair_n)
                unit(n, seg_n, 6, pair_n)
                project_out(a, 0, pair_a)
                project_out(a, 1)
                unit(n, seg_n, 7, pair_n)
                project_out(a, 2)
                project_out(a, 3)

            def late_step(a, seg, s):
                n, odd = a + 1, seg % 2
                wait(pe, xlo_done, TILES + CH * s)
                transposes_and_scores(a, 0)
                unit(n, seg + 1, 0)
                sums_of_squares(s, yp[0])
                transposes_and_scores(a, 1)
                unit(n, seg + 1, 1)
                contributions(a, odd, 0)
                contributions(a, odd, 1)
                unit(n, seg + 1, 2)
                unit(n, seg + 1, 3)
                attend(a, odd, 0)
                attend(a, odd, 1)
                unit(n, seg + 1, 4)
                unit(n, seg + 1, 5)
                mid_transposes(s, (0, 1))
                unit(n, seg + 1, 6)
                mid_transposes(s, (2, 3))
                pe.wait_ge(rms_ready, s + 1)
                project_out(a, 0)
                project_out(a, 1)
                unit(n, seg + 1, 7)
                project_out(a, 2)
                project_out(a, 3)

            pe.wait_ge(const_done, 3)
            for t in range(CH):
                transpose_x(t, y[:, t], ln1_ring[t], t + 1)
            pe.wait_ge(xlo_done, CH)
            for s in range(1, NSEG):
                unit(0, 0, 2 * s - 2, 0)
                unit(0, 0, 2 * s - 1, 0)
                for t in range(s * CH, (s + 1) * CH):
                    wait(pe, xlo_done, t - 5)
                    transpose_x(t, y[:, t], ln1_ring[t % 6], t + 1)
            unit(0, 0, 6, 0)
            unit(0, 0, 7, 0)
            pe.wait_ge(xlo_done, TILES)
            step(0, 0, 1, pair_a=0)
            with pe.Fori(0, PAIRS - 1) as i:
                for j in range(NSEG):
                    a = 4 * i + 1 + j
                    step(a, (1 + j) % NSEG, a + 1, pair_n=i + 1 if j == 2 else None,
                         pair_a=i + 1 if j == 3 else None)
            late_step(STEPS - 3, 1, 0)
            late_step(STEPS - 2, 2, 1)

            def ffn_unit(narrow, m, seg, u, new_group=None, psum=ffn_ps):
                t, up = u // 2, u % 2
                if new_group is not None and up == 0:
                    pe.wait_ge(flo_done, 2 * new_group + t + 1)
                wait(pe, hid_done, 2 * (m - 1) + t + 1)
                split_product(psum[u][:, :],
                              [(f_hi[:, t, up, r], f_lo[:, t, up, r]) for r in range(HT)],
                              [(x_hi[:, r, tokens(seg)], x_lo[:, r, tokens(seg)]) for r in range(HT)],
                              fproj_done, "stationary" if narrow else None)

            def project_down(narrow, d, par, t, new_group=None):
                if t == 0:
                    pe.wait_ge(hlo_done, 2 * d + 2)
                    if new_group is not None:
                        pe.wait_ge(dlo_done, new_group + 1)
                if isinstance(d, int) and d == 0:
                    pe.wait_ge(yacc_done, 4 * STEPS)
                wait(pe, y2acc_done, 4 * d + t - 1)
                split_product(yp[t % 2][:, :],
                              [(h_hi[par][:, f, chunk(t)], h_lo[par][:, f, chunk(t)]) for f in range(2)],
                              [(d_hi[:, f], d_lo[:, f]) for f in range(2)],
                              down_done, "moving" if narrow else None)

            def ffn_step(narrow, m, seg, d, par, new_group=None, down_group=None):
                for t in range(2):
                    for u in range(2):
                        ffn_unit(narrow, m, seg, 2 * t + u, new_group)
                    for u in range(2):
                        project_down(narrow, d, par, 2 * t + u, down_group)

            def last_step_and_ffn(narrow):
                def project(m, t, psum=ffn_ps):
                    for u in range(2):
                        ffn_unit(narrow, m, m % NSEG, 2 * t + u, 0 if m == 0 else None, psum)

                def down(d, tiles=range(CH)):
                    for t in tiles:
                        project_down(narrow, d, d % 2, t, 0 if d == 0 else None)

                last = STEPS - 1
                pe.wait_ge(xlo_done, TILES + 2 * CH)
                transposes_and_scores(last, 0)
                sums_of_squares(2, yp[0])
                pe.wait_ge(sig_done, 8 * STEPS)
                project(0, 0, ffn_ps_first)
                transposes_and_scores(last, 1)
                contributions(last, 1, 0)
                contributions(last, 1, 1)
                pe.wait_ge(rms_ready, 3)
                pe.wait_ge(yacc_done, 4 * last)
                project(0, 1, ffn_ps_first)
                attend(last, 1, 0)
                attend(last, 1, 1)
                project(1, 0)
                sums_of_squares(3, sc_st[0])
                pe.wait_ge(gated_done, 2 * STEPS)
                project(1, 1)
                pe.wait_ge(hid_done, 2)
                for t in range(CH):
                    project_out(last, t)
                pe.wait_ge(rms_ready, NSEG)
                mid_transposes(2, (0, 1))
                down(0)
                mid_transposes(2, (2, 3))
                pe.wait_ge(xlo_done, TILES + 3 * CH)
                project(2, 0)
                project(2, 1)
                down(1)
                mid_transposes(3, (0, 1))
                down(2, (0, 1))
                mid_transposes(3, (2, 3))
                down(2, (2, 3))
                pe.wait_ge(xlo_done, 2 * TILES)
                project(3, 0)
                project(3, 1)
                with pe.Fori(1, FG - 1) as i:
                    for j in range(NSEG):
                        m = 4 * i + j
                        ffn_step(narrow, m, j, m - 1, (j + 1) % 2,
                                 new_group=i if j == 0 else None, down_group=i if j == 1 else None)
                for j in range(NSEG - 1):
                    m = FSTEPS - NSEG + j
                    ffn_step(narrow, m, j, m - 1, (j + 1) % 2,
                             new_group=FG - 1 if j == 0 else None,
                             down_group=FG - 1 if j == 1 else None)
                project(FSTEPS - 1, 0)
                project(FSTEPS - 1, 1)
                down(FSTEPS - 2)
                down(FSTEPS - 1)

            pe.wait_ge(wide_ready, 1)
            needs_lo = pe.value_load(wide[0:1, 0:1], min_val=0, max_val=1)
            with pe.If(needs_lo == 1):
                last_step_and_ffn(False)
            with pe.Else():
                last_step_and_ffn(True)


def decay_tables(np):
    layer, layers = 1, 32
    base = np.float32(1.0 / 2.0 ** (8.0 / HEADS))
    factor = np.float32(1.0 - layer / (layers - 1 + 1e-05) + 1e-05)
    slope = (base ** (np.arange(HEADS, dtype=np.float32) + np.float32(1)) * factor).astype(np.float32)
    r = np.arange(P, dtype=np.float32) + np.float32(1)
    t = np.zeros((PAIRS, P, TAB), np.float32)
    for head in range(HEADS):
        p, h, s = head // 2, head % 2, slope[head]
        diff = r[None, :] - r[:, None]
        t[p, :, TAB_D + h * P:TAB_D + (h + 1) * P] = np.where(diff >= 0, np.exp(-s * np.abs(diff)), 0)
        t[p, :, TAB_Q + h * P:TAB_Q + (h + 1) * P] = np.exp(-s * r)[None, :]
        t[p, :, TAB_K + h] = np.exp(-s * (np.float32(P) - r))
        t[p, :, TAB_B + h] = np.exp(-s * np.float32(P))
    return t


def kernel(L0_attn_hidden_states, L0_attn_qkv_w, L0_attn_out_w, L0_attn_gate_w, L0_attn_norm_w,
           L0_ffn_gate_t, L0_ffn_up_t, L0_ffn_down_t, L0_ffn_gate_s, L0_ffn_up_s, L0_ffn_down_s):
    import numpy as np
    import concourse.bacc as bacc
    from concourse.bass_utils import run_bass_kernel_spmd

    qkv = np.asarray(L0_attn_qkv_w).reshape(PAIRS, 2, 3, HD, HT, P)
    gate = np.asarray(L0_attn_gate_w).reshape(PAIRS, 2, 1, HD, HT, P)
    w = np.concatenate([qkv[:, :, 1:2], qkv[:, :, 0:1], qkv[:, :, 2:3], gate], axis=2)
    w_attn = w.transpose(0, 2, 5, 4, 1, 3)
    w_out = np.asarray(L0_attn_out_w).reshape(HID, PAIRS, 2, HD).transpose(1, 3, 2, 0)
    norm_w = np.asarray(L0_attn_norm_w).reshape(PAIRS, 2, HD).transpose(0, 2, 1)
    gu = np.stack([np.asarray(L0_ffn_gate_t), np.asarray(L0_ffn_up_t)]).reshape(2, FG, 2, P, HT, P)
    w_ffn = gu.transpose(1, 5, 2, 0, 4, 3)
    w_down = np.asarray(L0_ffn_down_t).reshape(HID, FG, 2, P).transpose(1, 3, 2, 0)
    scales = np.stack([np.asarray(L0_ffn_gate_s), np.asarray(L0_ffn_up_s)]).reshape(2, FG, 2, P)
    arrays = {
        "x": np.asarray(L0_attn_hidden_states).reshape(TOK, HID),
        "w_attn": w_attn, "w_out": w_out, "norm_w": norm_w, "tables": decay_tables(np),
        "w_ints": np.concatenate([w_ffn.ravel(), w_down.ravel()]),
        "ffn_scales": scales.transpose(1, 3, 0, 2).reshape(FG, P, 4),
        "down_s": np.asarray(L0_ffn_down_s),
    }
    arrays = {name: np.ascontiguousarray(a) for name, a in arrays.items()}
    nc = bacc.Bacc("TRN2", target_bir_lowering=False, num_devices=1)
    aps = [nc.dram_tensor(name, a.shape, mybir.dt.from_np(a.dtype), kind="ExternalInput").ap()
           for name, a in arrays.items()]
    out = nc.dram_tensor("out", (TOK, HID), F32, kind="ExternalOutput").ap()
    sandwich_kernel(nc, *aps, out)
    result = run_bass_kernel_spmd(nc, [arrays], core_ids=[0])
    return result.results[0]["out"].reshape(BATCH, SEQ, HID)
```
